# Optimizing a Trainium2 kernel written in Bass

```python
import numpy as np
import jax
import jax.numpy as jnp

def _softmax(x, axis=-1):
    return jax.nn.softmax(x, axis=axis)

def _gelu(x):
    return jax.nn.gelu(x, approximate=True)

def _silu(x):
    return jax.nn.silu(x)

def _sigmoid(x):
    return jax.nn.sigmoid(x)

def _layernorm(x, axis=-1, eps=1e-05):
    m = jnp.mean(x, axis=axis, keepdims=True)
    v = jnp.var(x, axis=axis, keepdims=True)
    return (x - m) / jnp.sqrt(v + eps)

def _scatter_add(tgt, idx, src, axis=0):
    return tgt.at[idx].add(src)

def _segment_sum(src, seg, n):
    return jax.ops.segment_sum(src, seg, n)
kernel_name = 'mk_adaln_d1_jaxref_r8_b235f4'

def setup_inputs(seed: int=0):
    np.random.seed(seed)
    _w = jnp.asarray

    def _L0_attn_setup():
        import jax, jax.numpy as jnp
        import numpy as np
        DIM = 128
        HEADS = 16
        DIM_HEAD = 64
        key = jax.random.key(seed)
        ks = jax.random.split(key, 6)
        inner = HEADS * DIM_HEAD
        s = lambda fan_in: 1.0 / np.sqrt(fan_in)
        return {'x': jax.random.normal(ks[0], (4, 512, DIM), dtype=jnp.float32), 'W_qkv': jax.random.normal(ks[1], (DIM, inner * 3), dtype=jnp.float32) * s(DIM), 'W_f': jax.random.normal(ks[2], (DIM_HEAD, DIM_HEAD), dtype=jnp.float32) * s(DIM_HEAD), 'b_f': jax.random.normal(ks[3], (DIM_HEAD,), dtype=jnp.float32) * 0.01, 'W_out': jax.random.normal(ks[4], (inner, DIM), dtype=jnp.float32) * s(inner), 'b_out': jax.random.normal(ks[5], (DIM,), dtype=jnp.float32) * 0.01}
    _L0_attn_in = _L0_attn_setup()

    def _L0_ffn_setup():
        import jax, jax.numpy as jnp
        import numpy as np
        D_MODEL = 128
        D_FFN = 256
        N_EXPERTS = 8
        TOP_K = 2
        B, S = (2, 256)
        LN_EPS = 1e-05
        key = jax.random.key(seed)
        ks = jax.random.split(key, 6)
        scale = 0.02
        x = jax.random.normal(ks[0], (B, S, D_MODEL), dtype=jnp.float32)
        w_router = jax.random.normal(ks[1], (N_EXPERTS, D_MODEL), dtype=jnp.float32) * scale
        w_gate = jax.random.normal(ks[2], (N_EXPERTS, D_FFN, D_MODEL), dtype=jnp.float32) * scale
        w_up = jax.random.normal(ks[3], (N_EXPERTS, D_FFN, D_MODEL), dtype=jnp.float32) * scale
        w_down = jax.random.normal(ks[4], (N_EXPERTS, D_MODEL, D_FFN), dtype=jnp.float32) * scale
        ln_gamma = jnp.ones((D_MODEL,), dtype=jnp.float32)
        ln_beta = jnp.zeros((D_MODEL,), dtype=jnp.float32)
        return {'x': x, 'w_router': w_router, 'w_gate': w_gate, 'w_up': w_up, 'w_down': w_down, 'ln_gamma': ln_gamma, 'ln_beta': ln_beta}
    _L0_ffn_in = _L0_ffn_setup()
    _L0_c = _w((lambda *s: np.random.randn(*s).astype(np.float32) * 0.05)(4, 128))
    _L0_wmod = _w((lambda *s: np.random.randn(*s).astype(np.float32) * 0.05)(128, 6 * 128) * 128 ** (-0.5))
    _d = {'L0_attn_x': _L0_attn_in['x'], 'L0_attn_W_qkv': _L0_attn_in['W_qkv'], 'L0_attn_W_f': _L0_attn_in['W_f'], 'L0_attn_b_f': _L0_attn_in['b_f'], 'L0_attn_W_out': _L0_attn_in['W_out'], 'L0_attn_b_out': _L0_attn_in['b_out'], 'L0_ffn_w_router': _L0_ffn_in['w_router'], 'L0_ffn_w_gate': _L0_ffn_in['w_gate'], 'L0_ffn_w_up': _L0_ffn_in['w_up'], 'L0_ffn_w_down': _L0_ffn_in['w_down'], 'L0_ffn_ln_gamma': _L0_ffn_in['ln_gamma'], 'L0_ffn_ln_beta': _L0_ffn_in['ln_beta'], 'L0_c': _L0_c, 'L0_wmod': _L0_wmod}
    _x0 = _d['L0_attn_x']
    _d['L0_attn_x'] = jax.random.normal(jax.random.fold_in(jax.random.key(seed), 1), (4, 1024, 128), dtype=_x0.dtype)
    del _x0
    return _d

def reference(L0_attn_x, L0_attn_W_qkv, L0_attn_W_f, L0_attn_b_f, L0_attn_W_out, L0_attn_b_out, L0_ffn_w_router, L0_ffn_w_gate, L0_ffn_w_up, L0_ffn_w_down, L0_ffn_ln_gamma, L0_ffn_ln_beta, L0_c, L0_wmod):

    def _L0_attn_ref(x, W_qkv, W_f, b_f, W_out, b_out):
        import jax, jax.numpy as jnp
        import numpy as np
        DIM = 128
        HEADS = 16
        DIM_HEAD = 64
        B, N, C = x.shape
        H, D = (HEADS, DIM_HEAD)
        qkv = x @ W_qkv
        q, k, v = jnp.split(qkv, 3, axis=-1)
        reshape = lambda t: t.reshape(B, N, H, D).transpose(0, 2, 1, 3)
        q, k, v = (reshape(q), reshape(k), reshape(v))
        fmap = lambda t: jax.nn.relu(t @ W_f + b_f)
        q = fmap(q)
        k = fmap(k)
        kv = jnp.einsum('bhnd,bhne->bhde', k, v)
        out = jnp.einsum('bhnd,bhde->bhne', q, kv)
        k_sum = k.sum(axis=2)
        normalizer = jnp.einsum('bhnd,bhd->bhn', q, k_sum)
        out = out / (normalizer[..., None] + 1e-06)
        out = out.transpose(0, 2, 1, 3).reshape(B, N, H * D)
        return out @ W_out + b_out

    def _L0_ffn_ref(x, w_router, w_gate, w_up, w_down, ln_gamma, ln_beta):
        import jax, jax.numpy as jnp
        import numpy as np
        D_MODEL = 128
        D_FFN = 256
        N_EXPERTS = 8
        TOP_K = 2
        B, S = (2, 256)
        LN_EPS = 1e-05
        logits = jnp.einsum('bsd,ed->bse', x, w_router)
        top_vals, top_idx = jax.lax.top_k(logits, TOP_K)
        rw = jax.nn.softmax(top_vals, axis=-1)
        gate = jnp.einsum('bsd,efd->ebsf', x, w_gate)
        up = jnp.einsum('bsd,efd->ebsf', x, w_up)
        h = jax.nn.silu(gate) * up
        y = jnp.einsum('ebsf,edf->bsed', h, w_down)
        sel = jnp.take_along_axis(y, top_idx[..., None], axis=2)
        out = jnp.sum(rw[..., None] * sel, axis=2)
        mu = jnp.mean(out, axis=-1, keepdims=True)
        var = jnp.mean(jnp.square(out - mu), axis=-1, keepdims=True)
        out = (out - mu) * jax.lax.rsqrt(var + LN_EPS)
        return out * ln_gamma + ln_beta
    x = L0_attn_x
    mod = (_silu(L0_c) @ L0_wmod).reshape(L0_c.shape[0], 6, 1, -1)
    sa, ca, ga, sb, cb, gb = (mod[:, 0], mod[:, 1], mod[:, 2], mod[:, 3], mod[:, 4], mod[:, 5])
    ga = (2 * (ga >= 0) - 1) * jnp.maximum(jnp.abs(ga), 0.25)
    gb = (2 * (gb >= 0) - 1) * jnp.maximum(jnp.abs(gb), 0.25)
    h = _layernorm(x, axis=-1) * (1 + ca) + sa
    x = x + ga * _L0_attn_ref(h, L0_attn_W_qkv, L0_attn_W_f, L0_attn_b_f, L0_attn_W_out, L0_attn_b_out)
    h = _layernorm(x, axis=-1) * (1 + cb) + sb
    x = x + gb * _L0_ffn_ref(h, L0_ffn_w_router, L0_ffn_w_gate, L0_ffn_w_up, L0_ffn_w_down, L0_ffn_ln_gamma, L0_ffn_ln_beta)
    return x

_drawn_inputs = setup_inputs


def setup_inputs(seed=0):
    import zlib

    import numpy as np

    out = dict(_drawn_inputs(seed))
    spreads = {'L0_ffn_ln_gamma': (1.0, 0.2), 'L0_ffn_ln_beta': (0.0, 0.324)}
    factors = {'L0_attn_W_f': 3.586, 'L0_attn_b_f': 8.0, 'L0_attn_b_out': 4.715}
    for name, (base, spread) in spreads.items():
        noise = np.random.default_rng([zlib.crc32(name.encode()), seed]).standard_normal(out[name].shape)
        drawn = base * np.exp(spread * noise) if base else spread * noise
        out[name] = jnp.asarray(drawn.astype(out[name].dtype))
    for name, factor in factors.items():
        out[name] = (out[name] * factor).astype(out[name].dtype)
    return out
```

```python
from contextlib import ExitStack

import concourse.bass as bass
from concourse import mybir

ALU = mybir.AluOpType
ACT = mybir.ActivationFunctionType
F32 = mybir.dt.float32
F32R = mybir.dt.float32r
BF16 = mybir.dt.bfloat16
U32 = mybir.dt.uint32
AX_X = mybir.AxisListType.X
P = 128


def build_block(nc, x, wqkv, wf, bf, wout, bout, wrouter, wgate, wup, wdown, gamma, beta, cond, wmod, out):
    B, N, C = x.shape
    D = wf.shape[0]
    INNER = wout.shape[0]
    H = INNER // D
    E, F, _ = wgate.shape
    T = N // P
    G = T // 4
    NJ = INNER // P
    S = (2 * N + E * (P - 1)) // P
    NQ = (S + 3) // 4
    EPS = 1e-5
    BIG = 3.0e38
    assert C == P and D == 64 and H == 2 * NJ and F == 2 * P and T == 8 and E == 8 and G == 2

    ctx = ExitStack()
    with ctx:
        def sb(name, shape, dt=F32):
            return ctx.enter_context(nc.sbuf_tensor(name, shape, dt))

        def sem(name):
            return ctx.enter_context(nc.semaphore(name))

        ident = sb("ident", [P, P])
        lower_bf = sb("lower_bf", [P, P], BF16)
        ones_bf = sb("ones_bf", [P, P], BF16)
        ones_col = sb("ones_col", [P, 1])
        sel = sb("sel", [P, NJ, P], F32R)
        head_mask = sb("head_mask", [P, NJ, H])
        iota_e = sb("iota_e", [P, T, E])
        step128 = sb("step128", [P, E, T])
        before = sb("before", [P, E, E])
        iota_s = sb("iota_s", [P, S, E])
        neg_half = sb("neg_half", [P, T])
        nothing = sb("nothing", [P, 1])

        wqk_hi = sb("wqk_hi", [P, 2, INNER], F32R)
        wqk_lo = sb("wqk_lo", [P, 2, INNER], F32R)
        vo = sb("vo", [P, H, P])
        wgu_hi = sb("wgu_hi", [P, E * 2 * F], F32R)
        wgu_lo = sb("wgu_lo", [P, E * 2 * F], F32R)
        wd = sb("wd", [P, E * 2 * P])
        wr_t = sb("wr_t", [P, E])
        bf_col = sb("bf_col", [P, 1])
        bf_row = sb("bf_row", [P, D])
        bout_row = sb("bout_row", [P, P])
        gamma_row = sb("gamma_row", [P, P])
        beta_row = sb("beta_row", [P, P])
        mod = sb("mod", [P, B * 6 * P])
        fin = sb("fin", [P, B * 2 * P])

        q_act = sb("q_act", [P, G, NJ, 4 * P])
        flat = q_act[:, :, :, :].rearrange("p g j n -> p (g j n)")
        wqkv_nat = flat[:, 0:3 * INNER]
        wg_nat = flat[:, 3072:5120].rearrange("p (k c) -> p k c", c=P)
        wu_nat = flat[:, 5120:7168].rearrange("p (k c) -> p k c", c=P)
        hs = sb("hs", [P, S, P])
        y_sb = hs
        arena_k = sb("arena_k", [P, 3 * INNER])
        arena_x = sb("arena_x", [P, 2 * INNER])
        arena_a = sb("arena_a", [P, 2 * INNER])
        arena_t = sb("arena_t", [P, 2 * INNER])
        wd_nat = arena_a[:, :].rearrange("p (e f) -> p e f", e=E)
        wt = arena_k[:, :].rearrange("p (k c) -> p k c", c=P)
        wo_bd = arena_x[:, :].rearrange("p (j c) -> p j c", c=2 * P)
        sel_f = arena_t[:, 0:INNER].rearrange("p (j c) -> p j c", c=P)
        wf_bd = sb("wf_bd", [P, P])
        c_nat = sb("c_nat", [B, P])
        c_t = sb("c_t", [P, B])
        wmod_sb = arena_t[:, INNER:INNER + 6 * P]
        wr_nat = sb("wr_nat", [E, P])

        x_sb = arena_x[:, 0:INNER].rearrange("p (t c) -> p t c", c=P)
        h_sb = arena_x[:, INNER:2 * INNER].rearrange("p (t c) -> p t c", c=P)
        ht_hi = sb("ht_hi", [P, T * P], F32R)
        ht_lo = sb("ht_lo", [P, T * P], F32R)
        kf = arena_k[:, 0:2 * INNER].rearrange("p (a n) -> p a n", a=2)
        k_sum = arena_k[:, 2 * INNER:3 * INNER]
        gt_sb = sb("gt_sb", [P, INNER])
        ks_bd = sb("ks_bd", [P, NJ, H])
        m_sb = sb("m_sb", [P, NJ, P])
        norm_sb = sb("norm_sb", [H, 4 * P])
        recip_in = sb("recip_in", [P, 4, H])
        recip = sb("recip", [P, 4, P])
        r_parts = sb("r_parts", [P, 4 * P], F32R)
        c_b = recip
        qn = arena_a[:, 0:INNER].rearrange("p (a n) -> p a n", a=2)
        at_sb = arena_a[:, INNER:2 * INNER].rearrange("p (a n) -> p a n", a=2)
        tmp = arena_t[:, 0:INNER].rearrange("p (t c) -> p t c", c=P)
        x2 = arena_t[:, INNER:2 * INNER].rearrange("p (t c) -> p t c", c=P)

        def late(o, k, n):
            return flat[:, o:o + k * n].rearrange("p (k n) -> p k n", n=n)
        h2 = late(0, T, P)
        h2t = flat[:, 1024:2048]
        stats = sb("stats", [P, T, 6])
        mv = sb("mv", [P, T, 2])
        var_e = sb("var_e", [P, T])
        rstd = sb("rstd", [P, T])
        logit = sb("logit", [P, T, E])
        code = sb("code", [P, T, E])
        eq = sb("eq", [P, T, E])
        pick1 = sb("pick1", [P, T, E])
        pick2 = sb("pick2", [P, T, E])
        picks_bf = sb("picks_bf", [P, 2 * T - 1, E], BF16)
        top1 = sb("top1", [P, T])
        top2 = sb("top2", [P, T])
        first = sb("first", [P, T])
        gap = sb("gap", [P, T])
        th = sb("th", [P, T])
        w1 = sb("w1", [P, T])
        w2 = sb("w2", [P, T])
        over = sb("over", [P, E, T])
        n_tiles = sb("n_tiles", [P, E])
        prior = sb("prior", [P, E, E])
        tile0 = sb("tile0", [P, E])
        tile1 = sb("tile1", [P, E])
        passed = sb("passed", [P, S, E])
        owner = sb("owner", [P, S])
        owner_i = sb("owner_i", [P, S], U32)
        slot = sb("slot", [P, T, E])
        slot_p = sb("slot_p", [P, T, E])
        slots = sb("slots", [P, 2 * T])
        slots_i = sb("slots_i", [P, 2 * T], U32)
        hst_hi = sb("hst_hi", [P, 2, 4 * P], F32R)
        hst_lo = sb("hst_lo", [P, 2, 4 * P], F32R)
        gate = late(2048, 2, F)
        hid = late(2560, 2, F)
        hid_t = late(3072, 2, F)
        y1 = kf[:, 0, :].rearrange("p (t c) -> p t c", c=P)
        y2 = kf[:, 1, :].rearrange("p (t c) -> p t c", c=P)
        res = late(4096, T, P)

        bank = [ctx.enter_context(nc.psum_tensor(f"bank{i}", [P, 512], F32)) for i in range(8)]

        rows_in = nc.dram_tensor("rows_in", [S * P, P], F32, kind="Internal").ap()
        rows_out = nc.dram_tensor("rows_out", [S * P, P], F32, kind="Internal").ap()

        const_ready = sem("const_ready")
        zeroed = sem("zeroed")
        in_qkv, in_heads, in_gu, in_down, in_cond, in_rows = (
            sem(n) for n in ("in_qkv", "in_heads", "in_gu", "in_down", "in_cond", "in_rows"))
        su_full, su_act, su_dve = sem("su_full"), sem("su_act"), sem("su_dve")
        sel_ready, c_wide = sem("sel_ready"), sem("c_wide")
        held = sem("held")
        pool_chain = sem("pool_chain")
        dve_chain = sem("dve_chain")
        act_chain = sem("act_chain")
        names = """x_in x_free var1 rstd1 h_ready ht_full ht_act ht_dve k_full k_biased k_relu g_done k_added q_full
            q_ready gt_copied ksum_full ks_ready m_full m_act m_dve norm_full norm_copied normt_full r_ready
            rt_full r_hi r_lo rb_full qn_ready out_done at_copied att_full x2_ready var2 rstd2 h2_ready h2t_full
            h2t_copied logit_full gap_ready tanh_done picks_ready rank_full route_ready scattered
            ft_full ft_hi ft_lo gu_full silu_done hid_ready hidt_full hidt_copied y_full y_copied y_stored
            gathered var3 rstd3 res_ready stored owner_ready""".split()
        sm = {n: sem(n) for n in names}
        hs_in = [sem(f"hs_in{q}") for q in range(NQ)]

        def quad(q):
            return range(4 * q, min(4 * q + 4, S))

        block = ctx.enter_context(nc.Block())

        @block.sync
        def _(sp):
            sp.dma_start(wqkv_nat, wqkv).then_inc(in_qkv, 16)
            sp.wait_ge(zeroed, 2)
            for s in range(2):
                lo, hi = s * D, (s + 1) * D
                sp.dma_start(wf_bd[lo:hi, lo:hi], wf).then_inc(in_heads, 16)
                sp.dma_start(wo_bd[lo:hi, :, s * P:(s + 1) * P],
                             wout.rearrange("(j s e) d -> s e j d", s=2, e=D)[s]).then_inc(in_heads, 16)
                sp.dma_start(bf_col[lo:hi, :], bf.rearrange("(e a) -> e a", a=1)).then_inc(in_rows, 16)
            sp.dma_start(wg_nat, wgate.rearrange("e (k p) c -> p (e k) c", p=P)).then_inc(in_gu, 16)
            sp.dma_start(wu_nat, wup.rearrange("e (k p) c -> p (e k) c", p=P)).then_inc(in_gu, 16)
            sp.dma_start(wd_nat, wdown.rearrange("e d f -> d e f")).then_inc(in_down, 16)
            for row, src in ((bf_row, bf), (bout_row, bout), (gamma_row, gamma), (beta_row, beta)):
                sp.dma_start(row[:, :], src.partition_broadcast(P)).then_inc(in_rows, 16)
            sp.wait_ge(zeroed, 3)
            sp.dma_start(rows_in.rearrange("(s p) c -> p s c", p=P), hs[:, :, :]).then_inc(sm["stored"], 16)

            x_flat, out_flat = x.rearrange("b n c -> (b n c)"), out.rearrange("b n c -> (b n c)")
            with sp.Fori(0, B) as b:
                at_batch = bass.ds(sp.snap(b * (N * C)), N * C)
                sp.wait_ge(sm["x_free"], b + 1)
                sp.wait_ge(sm["stored"], b * 16 + 16)
                sp.dma_start(x_sb[:, :, :], x_flat[at_batch].rearrange("(t p c) -> p t c", p=P, c=C)).then_inc(sm["x_in"], 16)
                sp.wait_ge(sm["scattered"], b * (32 * T) + 32 * T)
                for q in range(NQ):
                    n = len(quad(q))
                    sp.dma_start(hs[:, 4 * q:4 * q + n, :],
                                 rows_in[4 * q * P:(4 * q + n) * P, :].rearrange("(s p) c -> p s c", p=P)
                                 ).then_inc(hs_in[q], 16)
                for q in range(NQ):
                    n = len(quad(q))
                    sp.wait_ge(sm["y_copied"], b * S + 4 * q + n)
                    sp.dma_start(rows_out[4 * q * P:(4 * q + n) * P, :].rearrange("(s p) c -> p s c", p=P),
                                 y_sb[:, 4 * q:4 * q + n, :]).then_inc(sm["y_stored"], 16)
                sp.wait_ge(sm["res_ready"], b + 1)
                sp.dma_start(out_flat[at_batch].rearrange("(t p c) -> p t c", p=P, c=C), res[:, :, :]).then_inc(sm["stored"], 16)
            sp.wait_ge(sm["stored"], 16 * B + 16)

        @block.gpsimd
        def _(pool):
            n = [0]

            def link(ins):
                n[0] += 1
                ins.then_inc(pool_chain, 1)
                pool.wait_ge(pool_chain, n[0])

            pool.memset(neg_half[:, :], -0.5)
            pool.memset(nothing[:, :], 0.0)
            pool.memset(wf_bd[:, :], 0.0).then_inc(zeroed, 1)
            pool.memset(wo_bd[:, :, :], 0.0).then_inc(zeroed, 1)
            pool.memset(hs[:, :, :], 0.0).then_inc(zeroed, 1)
            pool.memset(ident[:, :], 0.0)
            pool.memset(lower_bf[:, :], 1.0)
            pool.memset(ones_bf[:, :], 1.0)
            pool.memset(ones_col[:, :], 1.0)
            pool.memset(sel_f[:, :, :], 0.0)
            pool.memset(head_mask[:, :, :], 0.0)
            pool.memset(before[:, :, :], 1.0)
            link(pool.memset(iota_e[:, :, :], 0.0))

            def select(ap, compare, fill, base, pattern, per_row):
                link(pool.affine_select(out=ap, in_=ap, compare_op=compare, fill=fill, base=base,
                                        pattern=pattern, channel_multiplier=per_row))
            select(ident[:, :], ALU.not_equal, 1.0, 0, [[-1, P]], 1)
            select(lower_bf[:, :], ALU.is_gt, 0.0, 0, [[1, P]], -1)
            sel_v = sel_f[:, :, :].rearrange("p j (s e) -> p j s e", s=2)
            for base in (0, -32):
                select(sel_v, ALU.not_equal, 1.0, base, [[-2, NJ], [-1, 2], [0, D]], 1)
            for s in range(2):
                select(head_mask[s * D:(s + 1) * D, :, :], ALU.not_equal, 1.0, -s, [[-2, NJ], [1, H]], 0)
            select(before[:, :, :], ALU.is_gt, 0.0, 0, [[1, E], [-1, E]], 0)
            pool.iota(iota_e[:, :, :], [[0, T], [1, E]], base=0, channel_multiplier=0,
                      allow_small_or_imprecise_dtypes=True)
            pool.iota(step128[:, :, :], [[0, E], [P, T]], base=0, channel_multiplier=0,
                      allow_small_or_imprecise_dtypes=True)
            link(pool.iota(iota_s[:, :, :], [[1, S], [0, E]], base=0, channel_multiplier=0,
                           allow_small_or_imprecise_dtypes=True))
            pool.memset(ones_col[:, :], 1.0).then_inc(const_ready, 1)
            pool.wait_ge(sm["stored"], 16)

            def rsqrt(b, var, rstd_sem):
                pool.wait_ge(sm[var], b + 1)
                pool.tensor_tensor(rstd[:, :], var_e[:, :], neg_half[:, :], ALU.pow).then_inc(sm[rstd_sem], 1)

            def hold(name, value):
                pool.wait_ge(sm[name], value)
                pool.tensor_tensor(nothing[:, :], nothing[:, :], nothing[:, :], ALU.add).then_inc(held, 1)

            with pool.Fori(0, B) as b:
                rsqrt(b, "var1", "rstd1")
                for t in range(1, T):
                    pool.wait_ge(sm["k_relu"], b * 2 * T + 2 * t + 2)
                    if t >= 2:
                        pool.wait_ge(sm["k_added"], b * (T - 1) + t - 1)
                    pool.tensor_tensor(k_sum[:, :], kf[:, 0, :] if t == 1 else k_sum[:, :], kf[:, t % 2, :],
                                       ALU.add).then_inc(sm["k_added"], 1)
                rsqrt(b, "var2", "rstd2")
                hold("route_ready", b + 1)
                for t in range(T):
                    for k in range(2):
                        pool.indirect_dma_start(
                            out=rows_in, out_offset=bass.IndirectOffsetOnAxis(slots_i[:, k * T + t:k * T + t + 1], 0),
                            in_=h2[:, t, :], in_offset=None).then_inc(sm["scattered"], 16)
                pool.wait_ge(held, b * 2 + 1)
                hold("y_stored", b * (16 * NQ) + 16 * NQ)
                for t in range(T):
                    for k, y in enumerate((y1, y2)):
                        pool.indirect_dma_start(
                            out=y[:, t, :], out_offset=None, in_=rows_out,
                            in_offset=bass.IndirectOffsetOnAxis(slots_i[:, k * T + t:k * T + t + 1], 0),
                        ).then_inc(sm["gathered"], 16)
                pool.wait_ge(held, b * 2 + 2)
                rsqrt(b, "var3", "rstd3")

        @block.scalar
        def _(act):
            act.dma_start(c_nat[:, :], cond).then_inc(in_cond, 16)
            act.dma_start(wmod_sb[:, :], wmod).then_inc(in_cond, 16)
            act.dma_start(wr_nat[:, :], wrouter).then_inc(in_cond, 16)
            job = [0]

            def evac(dst):
                act.wait_ge(su_full, job[0] + 1)
                src = bank[job[0] % 8][:, 0:512]
                act.activation(dst, src, ACT.Copy).then_inc(su_act, 1)
                job[0] += 1

            act.wait_ge(su_full, 1)
            act.activation(wr_t[:, :], bank[0][:, 0:E], ACT.Copy)
            act.activation(c_t[:, :], bank[0][:, 16:16 + B], ACT.Silu).then_inc(su_act, 1)
            act.wait_ge(su_act, 1)
            for b in range(B):
                act.activation(c_b[:, b, :], c_t[:, b:b + 1].to_broadcast([P, P]), ACT.Copy).then_inc(c_wide, 1)
            job[0] = 1
            for k in range(6):
                evac(wt[:, 4 * k:4 * k + 4, :])
            for k in range(2 * B):
                evac_mod = mod[:, (k // 2) * 768 + (k % 2) * 384:(k // 2) * 768 + (k % 2) * 384 + 384]
                act.wait_ge(su_full, job[0] + 1)
                act.activation(evac_mod, bank[job[0] % 8][:, 0:384], ACT.Copy).then_inc(su_act, 1)
                job[0] += 1
            for k in range(4):
                evac(wqk_hi[:, k // 2, (k % 2) * 512:(k % 2) * 512 + 512])
            for k in range(4):
                evac(vo[:, 4 * k:4 * k + 4, :])
            for e in range(E):
                evac(wgu_hi[:, e * 512:e * 512 + 512])
            for k in range(4):
                evac(wd[:, k * 512:k * 512 + 512])

            with act.Fori(0, B) as b:
                for g in range(G):
                    act.wait_ge(sm["ht_full"], b * G + g + 1)
                    act.activation(ht_hi[:, g * 512:g * 512 + 512], bank[6 + g][:, :], ACT.Copy
                                   ).then_inc(sm["ht_act"], 1)
                for i in range(2 * T):
                    act.wait_ge(sm["k_biased"], b * 2 * T + i + 1)
                    half = kf[:, (i // 2) % 2, (i % 2) * 512:(i % 2) * 512 + 512]
                    act.activation(half, half, ACT.Relu).then_inc(sm["k_relu"], 1)

                def q_relu(g):
                    for j in range(NJ):
                        i = NJ * g + j
                        act.wait_ge(sm["q_full"], b * G * NJ + i + 1)
                        act.activation(q_act[:, g, j, :], bank[i % 2][:, :], ACT.Relu, bias=bf_col[:, 0:1]
                                       ).then_inc(sm["q_ready"], 1)

                act.wait_ge(sm["g_done"], b * T + T)
                for k in range(2):
                    act.activation(gt_sb[:, k * 512:k * 512 + 512], bank[2 + k][:, :], ACT.Copy
                                   ).then_inc(sm["gt_copied"], 1)
                q_relu(0)
                for k in range(4):
                    act.wait_ge(sm["m_full"], b * 4 + k + 1)
                    mb = bank[(4, 6, 2, 3)[k]][0:D, :].rearrange("p (a s d) -> p a s d", a=2, s=2)
                    act.activation(m_sb[0:D, 2 * k:2 * k + 2, :], mb[:, :, 0, :], ACT.Copy).then_inc(sm["m_act"], 1)

                def norms(g):
                    act.wait_ge(sm["norm_full"], b * G + g + 1)
                    act.activation(norm_sb[:, :], bank[5][0:H, :], ACT.Copy).then_inc(sm["norm_copied"], 1)

                def recips(g):
                    act.wait_ge(sm["rt_full"], b * G + g + 1)
                    act.activation(r_parts[:, :], bank[6][:, :], ACT.Copy).then_inc(sm["r_hi"], 1)

                norms(0)
                recips(0)
                q_relu(1)
                norms(1)
                for g in range(G):
                    if g:
                        recips(1)
                    act.wait_ge(sm["out_done"], b * G * NJ + NJ * (g + 1))
                    act.activation(at_sb[:, g, :], bank[4 + g][:, :], ACT.Copy).then_inc(sm["at_copied"], 1)
                for g in range(G):
                    act.wait_ge(sm["h2t_full"], b * G + g + 1)
                    act.activation(h2t[:, g * 512:g * 512 + 512], bank[6 + g][:, :], ACT.Copy
                                   ).then_inc(sm["h2t_copied"], 1)
                act.wait_ge(sm["gap_ready"], b + 1)
                act.activation(th[:, :], gap[:, :], ACT.Tanh, scale=0.5).then_inc(sm["tanh_done"], 1)

                def fhi(q):
                    w = len(quad(q)) * P
                    act.wait_ge(sm["ft_full"], b * NQ + q + 1)
                    if q >= 2:
                        act.wait_ge(sm["gu_full"], b * S + 4 * q - 4)
                    act.activation(hst_hi[:, q % 2, 0:w], bank[(7, 2)[q % 2]][:, 0:w], ACT.Copy
                                   ).then_inc(sm["ft_hi"], 1)

                fhi(0)
                for i in range(S + 1):
                    if i < S:
                        if i % 4 == 0 and i // 4 + 1 < NQ:
                            fhi(i // 4 + 1)
                        act.wait_ge(sm["gu_full"], b * S + i + 1)
                        if i >= 2:
                            act.wait_ge(sm["hid_ready"], b * S + i - 1)
                        act.activation(gate[:, i % 2, :], bank[i % 2][:, 0:F], ACT.Silu).then_inc(sm["silu_done"], 1)
                    if i >= 1:
                        act.wait_ge(sm["hidt_full"], b * S + i)
                        if i >= 3:
                            act.wait_ge(sm["y_full"], b * S + i - 2)
                        act.activation(hid_t[:, (i - 1) % 2, :], bank[(3, 6)[(i - 1) % 2]][:, 0:F], ACT.Copy
                                       ).then_inc(sm["hidt_copied"], 1)

        @block.vector
        def _(dve):
            n = [0]

            def link(ins):
                n[0] += 1
                ins.then_inc(dve_chain, 1)
                dve.wait_ge(dve_chain, n[0])

            def rows(ap2d, k=T):
                return ap2d.unsqueeze(1).to_broadcast([P, k, P])

            dve.wait_ge(const_ready, 1)
            dve.tensor_copy(sel[:, :, :], sel_f[:, :, :]).then_inc(sel_ready, 1)
            dve.wait_ge(sel_ready, 1)
            dve.wait_ge(in_rows, 16 * 6)
            dve.wait_ge(su_act, 1 + 6 + 2 * B)
            mod_v = mod[:, :].rearrange("p (b k c) -> p b k c", b=B, k=6)
            for k in (1, 4):
                dve.tensor_scalar(mod_v[:, :, k, :], mod_v[:, :, k, :], 1.0, None, ALU.add)
            t4 = tmp[:, 0:B, :]
            for k in (2, 5):
                link(dve.tensor_scalar(t4, mod_v[:, :, k, :], 0.0, 2.0, ALU.is_ge, ALU.mult))
                link(dve.tensor_scalar(t4, t4, -1.0, None, ALU.add))
                link(dve.tensor_tensor(mod_v[:, :, k, :], mod_v[:, :, k, :], t4, ALU.mult))
                link(dve.scalar_tensor_tensor(mod_v[:, :, k, :], mod_v[:, :, k, :], 0.25, t4, ALU.max, ALU.mult))
            fin_v = fin[:, :].rearrange("p (b k c) -> p b k c", b=B, k=2)
            dve.tensor_tensor(fin_v[:, :, 0, :], mod_v[:, :, 5, :], rows(gamma_row[:, :], B), ALU.mult)
            link(dve.tensor_tensor(fin_v[:, :, 1, :], mod_v[:, :, 5, :], rows(beta_row[:, :], B), ALU.mult))

            def rest(j, dst, hi):
                dve.wait_ge(su_act, j + 1)
                dve.tensor_tensor(dst, bank[j % 8][:, :], hi.bitcast(F32), ALU.subtract).then_inc(su_dve, 1)

            j0 = 1 + 6 + 2 * B
            for k in range(4):
                o = (k % 2) * 512
                rest(j0 + k, wqk_lo[:, k // 2, o:o + 512], wqk_hi[:, k // 2, o:o + 512])
            for e in range(E):
                rest(j0 + 8 + e, wgu_lo[:, e * 512:e * 512 + 512], wgu_hi[:, e * 512:e * 512 + 512])
            dve.memset(recip[:, :, :], 0.0)
            dve.memset(picks_bf[:, :, :], 0.0)
            dve.memset(top1[:, :], 0.0).then_inc(sm["x_free"], 1)

            def layer_norm(b, src, var, rstd_sem, dst, scale=None, shift=None, into=None, done=None):
                for t in range(T):
                    ins = dve.bn_stats(stats[:, t, :], src[:, t, :])
                link(ins)
                for t in range(T):
                    ins = dve.bn_aggr(mv[:, t, :], stats[:, t, :])
                link(ins)
                dve.tensor_scalar(var_e[:, :], mv[:, :, 1], EPS, None, ALU.add).then_inc(sm[var], 1)
                dve.wait_ge(sm[rstd_sem], b + 1)
                for t in range(T):
                    ins = dve.tensor_scalar(dst[:, t, :], src[:, t, :], mv[:, t, 0:1], rstd[:, t:t + 1],
                                            ALU.subtract, ALU.mult)
                link(ins)
                link(dve.tensor_tensor(dst[:, :, :], dst[:, :, :], scale, ALU.mult))
                dve.tensor_tensor(dst[:, :, :], dst[:, :, :], shift, ALU.add).then_inc(sm[done], 1)

            with dve.Fori(0, B) as b:
                dve.sem_clear(dve_chain)
                n[0] = 0

                def modrow(k, table=mod, width=6, tiles=T):
                    return rows(table[:, bass.ds(b * (width * P) + k * P, P)], tiles)

                dve.wait_ge(sm["x_in"], b * 16 + 16)
                layer_norm(b, x_sb, "var1", "rstd1", h_sb, modrow(1), modrow(0), done="h_ready")
                for g in range(G):
                    dve.wait_ge(sm["ht_act"], b * G + g + 1)
                    o = g * 512
                    dve.tensor_tensor(ht_lo[:, o:o + 512], bank[6 + g][:, :], ht_hi[:, o:o + 512].bitcast(F32),
                                      ALU.subtract).then_inc(sm["ht_dve"], 1)
                bias = bf_row[:, :].unsqueeze(1).to_broadcast([P, 512 // D, D])
                for i in range(2 * T):
                    t = i // 2
                    dve.wait_ge(sm["k_full"], b * 2 * T + i + 1)
                    if i % 2 == 0 and t >= 2:
                        dve.wait_ge(sm["g_done"], b * T + t - 1)
                        dve.wait_ge(sm["k_added"], b * (T - 1) + max(1, t - 2))
                    dst = kf[:, t % 2, (i % 2) * 512:(i % 2) * 512 + 512]
                    dve.tensor_tensor(dst.rearrange("p (h d) -> p h d", d=D),
                                      bank[i % 2][:, :].rearrange("p (h d) -> p h d", d=D), bias, ALU.add
                                      ).then_inc(sm["k_biased"], 1)
                dve.wait_ge(sm["ksum_full"], b + 1)
                dve.tensor_tensor(ks_bd[:, :, :], head_mask[:, :, :],
                                  bank[7][:, 0:NJ].unsqueeze(2).to_broadcast([P, NJ, H]), ALU.mult
                                  ).then_inc(sm["ks_ready"], 1)
                for k in range(4):
                    dve.wait_ge(sm["m_full"], b * 4 + k + 1)
                    mb = bank[(4, 6, 2, 3)[k]][D:P, :].rearrange("p (a s d) -> p a s d", a=2, s=2)
                    dve.tensor_copy(m_sb[D:P, 2 * k:2 * k + 2, :], mb[:, :, 1, :]).then_inc(sm["m_dve"], 1)

                def recips(g):
                    dve.wait_ge(sm["normt_full"], b * G + g + 1)
                    link(dve.tensor_scalar(recip_in[:, :, :],
                                           bank[7][:, 64:64 + 4 * H].rearrange("p (t h) -> p t h", h=H),
                                           1e-6, None, ALU.add))
                    link(dve.reciprocal(recip[:, :, 0:H], recip_in[:, :, :]))
                    dve.tensor_copy(recip[:, :, 32:32 + H], recip[:, :, 0:H]).then_inc(sm["r_ready"], 1)

                def recips_lo(g):
                    dve.wait_ge(sm["r_hi"], b * G + g + 1)
                    dve.tensor_tensor(r_parts[32:64, :], bank[6][32:64, :], r_parts[32:64, :].bitcast(F32),
                                      ALU.subtract).then_inc(sm["r_lo"], 1)

                recips(0)
                recips_lo(0)
                recips(1)
                for g in range(G):
                    if g:
                        recips_lo(1)
                    for j in range(NJ):
                        i = NJ * g + j
                        dve.wait_ge(sm["rb_full"], b * G * NJ + i + 1)
                        if i >= 2:
                            dve.wait_ge(sm["out_done"], b * G * NJ + i - 1)
                        dve.tensor_tensor(qn[:, i % 2, :], bank[2 + i % 2][:, :], q_act[:, g, j, :], ALU.mult
                                          ).then_inc(sm["qn_ready"], 1)
                for g in range(G):
                    dve.wait_ge(sm["att_full"], b * G + g + 1)
                    tg = tmp[:, 4 * g:4 * g + 4, :]
                    link(dve.tensor_tensor(tg, bank[6 + g][:, :].rearrange("p (t c) -> p t c", c=P),
                                           rows(bout_row[:, :], 4), ALU.add))
                    link(dve.tensor_tensor(tg, tg, modrow(2, tiles=4), ALU.mult))
                    dve.tensor_tensor(x2[:, 4 * g:4 * g + 4, :], tg, x_sb[:, 4 * g:4 * g + 4, :], ALU.add
                                      ).then_inc(sm["x2_ready"], 1)
                dve.wait_ge(sm["x2_ready"], b * G + G)
                link(dve.memset(top2[:, :], 0.0))
                dve.memset(top1[:, :], 0.0).then_inc(sm["x_free"], 1)
                layer_norm(b, x2, "var2", "rstd2", h2, modrow(4), modrow(3), done="h2_ready")

                def wide(ap, k=E):
                    return ap.unsqueeze(2).to_broadcast([P, ap.shape[1], k])

                dve.wait_ge(sm["logit_full"], b + 1)
                link(dve.tensor_copy(logit[:, :, :], bank[5][:, 0:T * E].rearrange("p (t e) -> p t e", e=E)))
                for top, pick in ((top1, pick1), (top2, pick2)):
                    link(dve.tensor_reduce(top[:, :], logit[:, :, :], AX_X, ALU.max))
                    link(dve.tensor_tensor(eq[:, :, :], logit[:, :, :], wide(top[:, :]), ALU.is_equal))
                    link(dve.scalar_tensor_tensor(code[:, :, :], eq[:, :, :], -float(E), iota_e[:, :, :],
                                                  ALU.mult, ALU.add))
                    link(dve.tensor_reduce(first[:, :], code[:, :, :], AX_X, ALU.min))
                    link(dve.tensor_tensor(pick[:, :, :], code[:, :, :], wide(first[:, :]), ALU.is_equal))
                    if top is top1:
                        link(dve.scalar_tensor_tensor(logit[:, :, :], pick[:, :, :], -BIG, logit[:, :, :],
                                                      ALU.mult, ALU.add))
                dve.tensor_tensor(gap[:, :], top2[:, :], top1[:, :], ALU.subtract).then_inc(sm["gap_ready"], 1)
                dve.tensor_tensor(picks_bf[:, T - 1:, :], pick1[:, :, :], pick2[:, :, :], ALU.add
                                  ).then_inc(sm["picks_ready"], 1)
                dve.wait_ge(sm["tanh_done"], b + 1)
                dve.tensor_scalar(w2[:, :], th[:, :], 0.5, 0.5, ALU.mult, ALU.add)
                dve.tensor_scalar(w1[:, :], th[:, :], -0.5, 0.5, ALU.mult, ALU.add)
                dve.wait_ge(sm["rank_full"], b + 1)
                count = bank[4][:, 0:E].unsqueeze(2).to_broadcast([P, E, T])
                link(dve.tensor_tensor(over[:, :, :], count, step128[:, :, :], ALU.is_gt))
                link(dve.tensor_reduce(n_tiles[:, :], over[:, :, :], AX_X, ALU.add))
                link(dve.tensor_tensor(prior[:, :, :], before[:, :, :],
                                       n_tiles[:, :].unsqueeze(1).to_broadcast([P, E, E]), ALU.mult))
                link(dve.tensor_reduce(tile0[:, :], prior[:, :, :], AX_X, ALU.add))
                link(dve.tensor_tensor(tile1[:, :], tile0[:, :], n_tiles[:, :], ALU.add))
                link(dve.tensor_tensor(passed[:, :, :], tile1[:, :].unsqueeze(1).to_broadcast([P, S, E]),
                                       iota_s[:, :, :], ALU.is_le))
                link(dve.tensor_reduce(owner[:, :], passed[:, :, :], AX_X, ALU.add))
                dve.tensor_scalar(owner_i[:, :], owner[:, :], float(E - 1), None, ALU.min
                                  ).then_inc(sm["owner_ready"], 1)
                link(dve.scalar_tensor_tensor(slot[:, :, :], tile0[:, :].unsqueeze(1).to_broadcast([P, T, E]),
                                              float(P), bank[5][:, 64:128].rearrange("p (t e) -> p t e", e=E),
                                              ALU.mult, ALU.add))
                for k, pick in enumerate((pick1, pick2)):
                    link(dve.tensor_tensor(slot_p[:, :, :], slot[:, :, :], pick[:, :, :], ALU.mult))
                    link(dve.tensor_reduce(slots[:, k * T:(k + 1) * T], slot_p[:, :, :], AX_X, ALU.add))
                dve.tensor_copy(slots_i[:, :], slots[:, :]).then_inc(sm["route_ready"], 1)

                def flo(q):
                    w = len(quad(q)) * P
                    dve.wait_ge(sm["ft_hi"], b * NQ + q + 1)
                    dve.tensor_tensor(hst_lo[:, q % 2, 0:w], bank[(7, 2)[q % 2]][:, 0:w],
                                      hst_hi[:, q % 2, 0:w].bitcast(F32), ALU.subtract).then_inc(sm["ft_lo"], 1)

                flo(0)
                for i in range(S + 2):
                    if i < S:
                        if i % 4 == 0 and i // 4 + 1 < NQ:
                            flo(i // 4 + 1)
                        dve.wait_ge(sm["silu_done"], b * S + i + 1)
                        if i >= 2:
                            dve.wait_ge(sm["hidt_full"], b * S + i - 1)
                        dve.tensor_tensor(hid[:, i % 2, :], bank[i % 2][:, F:2 * F], gate[:, i % 2, :], ALU.mult
                                          ).then_inc(sm["hid_ready"], 1)
                    if i >= 2:
                        dve.wait_ge(sm["y_full"], b * S + i - 1)
                        dve.tensor_copy(y_sb[:, i - 2, :], bank[4 + i % 2][:, 0:P]).then_inc(sm["y_copied"], 1)

                dve.wait_ge(sm["gathered"], b * (32 * T) + 32 * T)
                for t in range(T):
                    ins = dve.tensor_scalar(tmp[:, t, :], y1[:, t, :], w1[:, t:t + 1], None, ALU.mult)
                link(ins)
                for t in range(T):
                    ins = dve.scalar_tensor_tensor(tmp[:, t, :], y2[:, t, :], w2[:, t:t + 1], tmp[:, t, :],
                                                   ALU.mult, ALU.add)
                link(ins)
                for t in range(T):
                    ins = dve.bn_stats(stats[:, t, :], tmp[:, t, :])
                link(ins)
                for t in range(T):
                    ins = dve.bn_aggr(mv[:, t, :], stats[:, t, :])
                link(ins)
                dve.tensor_scalar(var_e[:, :], mv[:, :, 1], EPS, None, ALU.add).then_inc(sm["var3"], 1)
                dve.wait_ge(sm["rstd3"], b + 1)
                for t in range(T):
                    ins = dve.tensor_scalar(tmp[:, t, :], tmp[:, t, :], mv[:, t, 0:1], rstd[:, t:t + 1],
                                            ALU.subtract, ALU.mult)
                link(ins)
                link(dve.tensor_tensor(tmp[:, :, :], tmp[:, :, :], modrow(0, fin, 2), ALU.mult))
                link(dve.tensor_tensor(tmp[:, :, :], tmp[:, :, :], modrow(1, fin, 2), ALU.add))
                dve.tensor_tensor(res[:, :, :], tmp[:, :, :], x2[:, :, :], ALU.add).then_inc(sm["res_ready"], 1)

        @block.tensor
        def _(pe):
            job = [0]
            splits = []

            def take():
                k = job[0] - 8
                if k >= 0:
                    pe.wait_ge(su_act, k + 1)
                    if k in splits:
                        pe.wait_ge(su_dve, splits.index(k) + 1)
                job[0] += 1
                return bank[(job[0] - 1) % 8]

            pe.wait_ge(const_ready, 1)
            pe.wait_ge(in_cond, 48)
            bk = take()
            pe.transpose(bk[:, 0:E], wr_nat[:, :], ident[0:E, 0:E])
            pe.transpose(bk[:, 16:16 + B], c_nat[:, :], ident[0:B, 0:B]).then_inc(su_full, 1)
            pe.wait_ge(in_qkv, 16)
            for k in range(6):
                bk = take()
                for i in range(4):
                    o = (4 * k + i) * P
                    ins = pe.transpose(bk[:, i * P:(i + 1) * P], wqkv_nat[:, o:o + P], ident[:, :])
                ins.then_inc(su_full, 1)
            pe.wait_ge(c_wide, B)
            for k in range(2 * B):
                bk = take()
                o = (k % 2) * 384
                pe.matmul(bk[:, 0:384], c_b[:, k // 2, :], wmod_sb[:, o:o + 384], start=True, stop=True
                          ).then_inc(su_full, 1)
            pe.wait_ge(su_act, 7)
            pe.wait_ge(in_heads, 64)
            for k in range(4):
                splits.append(job[0])
                bk = take()
                for i in range(4):
                    ins = pe.matmul(bk[:, i * P:(i + 1) * P], wt[:, 4 * k + i, :], wf_bd[:, :], start=True, stop=True)
                ins.then_inc(su_full, 1)
            for k in range(4):
                bk = take()
                for i in range(2):
                    j = 2 * k + i
                    ins = pe.matmul(bk[:, i * 256:(i + 1) * 256], wt[:, 16 + j, :], wo_bd[:, j, :],
                                    start=True, stop=True)
                ins.then_inc(su_full, 1)
            pe.wait_ge(in_gu, 32)
            for e in range(E):
                splits.append(job[0])
                bk = take()
                for i in range(4):
                    src = (wg_nat, wu_nat)[i // 2][:, 2 * e + i % 2, :]
                    ins = pe.transpose(bk[:, i * P:(i + 1) * P], src, ident[:, :])
                ins.then_inc(su_full, 1)
            pe.wait_ge(in_down, 16)
            for k in range(4):
                bk = take()
                for i in range(4):
                    e, f = 2 * k + i // 2, i % 2
                    ins = pe.transpose(bk[:, i * P:(i + 1) * P], wd_nat[:, e, f * P:(f + 1) * P], ident[:, :])
                ins.then_inc(su_full, 1)
            pe.wait_ge(su_act, job[0])
            pe.wait_ge(su_dve, 4 + E)
            pe.wait_ge(sel_ready, 1)

            def product(dst, hi, lo, rhs_hi, rhs_lo):
                pe.matmul(dst, hi, rhs_hi, start=True, stop=False)
                pe.matmul(dst, hi, rhs_lo, start=False, stop=False)
                return pe.matmul(dst, lo, rhs_hi, start=False, stop=True)

            with pe.Fori(0, B) as b:
                def transposes(ready, src, full):
                    pe.wait_ge(sm[ready], b + 1)
                    for g in range(G):
                        for i in range(4):
                            ins = pe.transpose(bank[6 + g][:, i * P:(i + 1) * P], src[:, 4 * g + i, :], ident[:, :])
                        ins.then_inc(sm[full], 1)

                transposes("h_ready", h_sb, "ht_full")
                pe.wait_ge(sm["ht_dve"], b * G + G)
                for t in range(T + 1):
                    if t < T:
                        for k in range(2):
                            i = 2 * t + k
                            if i >= 2:
                                pe.wait_ge(sm["k_biased"], b * 2 * T + i - 1)
                            tok, o = slice(t * P, (t + 1) * P), slice(k * 512, k * 512 + 512)
                            product(bank[k][:, :], ht_hi[:, tok], ht_lo[:, tok], wqk_hi[:, 1, o], wqk_lo[:, 1, o]
                                    ).then_inc(sm["k_full"], 1)
                    if t >= 1:
                        pe.wait_ge(sm["k_relu"], b * 2 * T + 2 * t)
                        for k in range(2):
                            ins = pe.matmul(bank[2 + k][:, :], h_sb[:, t - 1, :],
                                            kf[:, (t - 1) % 2, k * 512:k * 512 + 512], start=t == 1, stop=t == T)
                        ins.then_inc(sm["g_done"], 1)

                def q_features(g):
                    for j in range(NJ):
                        i = NJ * g + j
                        if i >= 2:
                            pe.wait_ge(sm["q_ready"], b * G * NJ + i - 1)
                        f, tok = slice(j * P, (j + 1) * P), slice(g * 512, g * 512 + 512)
                        product(bank[i % 2][:, :], wqk_hi[:, 0, f], wqk_lo[:, 0, f], ht_hi[:, tok], ht_lo[:, tok]
                                ).then_inc(sm["q_full"], 1)

                q_features(0)
                pe.wait_ge(sm["k_added"], b * (T - 1) + T - 1)
                for j in range(NJ):
                    ins = pe.matmul(bank[7][:, j:j + 1], k_sum[:, j * P:(j + 1) * P], ones_col[:, :],
                                    start=True, stop=True)
                ins.then_inc(sm["ksum_full"], 1)
                pe.wait_ge(sm["gt_copied"], b * 2 + 2)
                for k in range(4):
                    for i in range(2):
                        j = 2 * k + i
                        ins = pe.matmul(bank[(4, 6, 2, 3)[k]][:, i * 256:(i + 1) * 256], gt_sb[:, j * P:(j + 1) * P],
                                        vo[:, 2 * j:2 * j + 2, :], start=True, stop=True)
                    ins.then_inc(sm["m_full"], 1)

                def norms(g):
                    for j in range(NJ):
                        pe.wait_ge(sm["q_ready"], b * G * NJ + NJ * g + j + 1)
                        ins = pe.matmul(bank[5][0:H, :], ks_bd[:, j, :], q_act[:, g, j, :], start=j == 0,
                                        stop=j == NJ - 1)
                    ins.then_inc(sm["norm_full"], 1)

                def norms_t(g):
                    pe.wait_ge(sm["norm_copied"], b * G + g + 1)
                    for i in range(4):
                        ins = pe.matmul(bank[7][:, 64 + H * i:64 + H * i + H], norm_sb[:, i * P:(i + 1) * P],
                                        ident[0:H, 0:H], start=True, stop=True)
                    ins.then_inc(sm["normt_full"], 1)

                def recips_t(g):
                    pe.wait_ge(sm["r_ready"], b * G + g + 1)
                    for i in range(4):
                        ins = pe.transpose(bank[6][:, i * P:(i + 1) * P], recip[:, i, :], ident[:, :])
                    ins.then_inc(sm["rt_full"], 1)

                def attend(g):
                    pe.wait_ge(sm["r_lo"], b * G + g + 1)
                    for j in range(NJ + 1):
                        if j < NJ:
                            i = NJ * g + j
                            if i >= 2:
                                pe.wait_ge(sm["qn_ready"], b * G * NJ + i - 1)
                            pe.matmul(bank[2 + i % 2][:, :], sel[:, j, :], r_parts[:, :], start=True, stop=True
                                      ).then_inc(sm["rb_full"], 1)
                        if j >= 1:
                            i = NJ * g + j - 1
                            pe.wait_ge(sm["qn_ready"], b * G * NJ + i + 1)
                            pe.matmul(bank[4 + g][:, :], m_sb[:, j - 1, :], qn[:, i % 2, :], start=j == 1,
                                      stop=j == NJ).then_inc(sm["out_done"], 1)

                pe.wait_ge(sm["ks_ready"], b + 1)
                norms(0)
                norms_t(0)
                pe.wait_ge(sm["m_act"], b * 4 + 4)
                pe.wait_ge(sm["m_dve"], b * 4 + 4)
                recips_t(0)
                q_features(1)
                pe.wait_ge(sm["norm_copied"], b * G + 1)
                norms(1)
                norms_t(1)
                attend(0)
                recips_t(1)
                pe.wait_ge(sm["norm_copied"], b * G + G)
                attend(1)
                for g in range(G):
                    pe.wait_ge(sm["at_copied"], b * G + g + 1)
                    for i in range(4):
                        ins = pe.transpose(bank[6 + g][:, i * P:(i + 1) * P], at_sb[:, g, i * P:(i + 1) * P],
                                           ident[:, :])
                    ins.then_inc(sm["att_full"], 1)
                transposes("h2_ready", h2, "h2t_full")
                pe.wait_ge(sm["h2t_copied"], b * G + G)
                for t in range(T):
                    ins = pe.matmul(bank[5][:, t * E:(t + 1) * E], h2t[:, t * P:(t + 1) * P], wr_t[:, :],
                                    start=True, stop=True)
                ins.then_inc(sm["logit_full"], 1)
                pe.wait_ge(sm["picks_ready"], b + 1)
                rank = bank[5][:, 64:128]
                pe.matmul(rank, lower_bf[:, :], picks_bf[:, T - 1:, :], start=True, stop=False)
                for back in range(1, T):
                    pe.matmul(rank, ones_bf[:, :], picks_bf[:, T - 1 - back:2 * T - 1 - back, :], start=False,
                              stop=back == T - 1)
                for t in range(T):
                    ins = pe.matmul(bank[4][:, 0:E], ones_bf[:, :], picks_bf[:, T - 1 + t, :], start=t == 0,
                                    stop=t == T - 1)
                ins.then_inc(sm["rank_full"], 1)

                def tokens_t(q):
                    pe.wait_ge(hs_in[q], b * 16 + 16)
                    if q >= 2:
                        pe.wait_ge(sm["ft_lo"], b * NQ + q - 1)
                    for i, s in enumerate(quad(q)):
                        ins = pe.transpose(bank[(7, 2)[q % 2]][:, i * P:(i + 1) * P], hs[:, s, :], ident[:, :])
                    ins.then_inc(sm["ft_full"], 1)

                tokens_t(0)
                pe.wait_ge(sm["owner_ready"], b + 1)
                expert = {}
                for i in range(S + 2):
                    if i < S:
                        if i % 4 == 0 and i // 4 + 1 < NQ:
                            tokens_t(i // 4 + 1)
                        e = pe.value_load(owner_i[0:1, i:i + 1], min_val=0, max_val=E - 1)
                        expert[i] = e
                        pe.wait_ge(sm["ft_lo"], b * NQ + i // 4 + 1)
                        if i >= 2:
                            pe.wait_ge(sm["hid_ready"], b * S + i - 1)
                        tok = slice((i % 4) * P, (i % 4 + 1) * P)
                        cols = bass.ds(e * (2 * F), 2 * F)
                        product(bank[i % 2][:, :], hst_hi[:, (i // 4) % 2, tok], hst_lo[:, (i // 4) % 2, tok],
                                wgu_hi[:, cols], wgu_lo[:, cols]).then_inc(sm["gu_full"], 1)
                    if 1 <= i <= S:
                        k = i - 1
                        pe.wait_ge(sm["hid_ready"], b * S + k + 1)
                        if k >= 2:
                            pe.wait_ge(sm["hidt_copied"], b * S + k - 1)
                        for f in range(2):
                            ins = pe.transpose(bank[(3, 6)[k % 2]][:, f * P:(f + 1) * P],
                                               hid[:, k % 2, f * P:(f + 1) * P], ident[:, :])
                        ins.then_inc(sm["hidt_full"], 1)
                    if i >= 2:
                        k = i - 2
                        pe.wait_ge(sm["hidt_copied"], b * S + k + 1)
                        if k >= 2:
                            pe.wait_ge(sm["y_copied"], b * S + k - 1)
                        for f in range(2):
                            ins = pe.matmul(bank[4 + k % 2][:, 0:P], hid_t[:, k % 2, f * P:(f + 1) * P],
                                            wd[:, bass.ds(expert[k] * (2 * P) + f * P, P)], start=f == 0, stop=f == 1)
                        ins.then_inc(sm["y_full"], 1)


_INS = ['L0_attn_x', 'L0_attn_W_qkv', 'L0_attn_W_f', 'L0_attn_b_f', 'L0_attn_W_out', 'L0_attn_b_out',
        'L0_ffn_w_router', 'L0_ffn_w_gate', 'L0_ffn_w_up', 'L0_ffn_w_down', 'L0_ffn_ln_gamma', 'L0_ffn_ln_beta',
        'L0_c', 'L0_wmod']


def kernel(**inputs):
    import numpy as np
    import concourse.bacc as bacc
    from concourse import mybir as mb
    from concourse.bass_utils import run_bass_kernel_spmd

    nc = bacc.Bacc("TRN2", target_bir_lowering=False, num_devices=1)
    arrays, args = {}, []
    for name in _INS:
        a = np.ascontiguousarray(inputs[name])
        arrays[f"in_{name}"] = a
        args.append(nc.dram_tensor(f"in_{name}", a.shape, mb.dt.from_np(a.dtype), kind="ExternalInput").ap())
    shape = inputs['L0_attn_x'].shape
    args.append(nc.dram_tensor("out_x", shape, mb.dt.float32, kind="ExternalOutput").ap())
    build_block(nc, *args)
    r = run_bass_kernel_spmd(nc, [arrays], core_ids=[0])
    return r.results[0]["out_x"]
```

```python
from contextlib import ExitStack

import concourse.bass as bass
from concourse import mybir

ALU = mybir.AluOpType
ACT = mybir.ActivationFunctionType
F32 = mybir.dt.float32
F32R = mybir.dt.float32r
BF16 = mybir.dt.bfloat16
U32 = mybir.dt.uint32
AX_X = mybir.AxisListType.X
P = 128


def build_block(nc, x, wqkv, wf, bf, wout, bout, wrouter, wgate, wup, wdown, gamma, beta, cond, wmod, out):
    B, N, C = x.shape
    D = wf.shape[0]
    INNER = wout.shape[0]
    H = INNER // D
    E, F, _ = wgate.shape
    T = N // P
    G = T // 4
    NJ = INNER // P
    S = (2 * N + E * (P - 1)) // P
    NQ = (S + 3) // 4
    EPS = 1e-5
    BIG = 3.0e38
    assert C == P and D == 64 and H == 2 * NJ and F == 2 * P and T == 8 and E == 8 and G == 2

    ctx = ExitStack()
    with ctx:
        def sb(name, shape, dt=F32):
            return ctx.enter_context(nc.sbuf_tensor(name, shape, dt))

        def sem(name):
            return ctx.enter_context(nc.semaphore(name))

        ident = sb("ident", [P, P])
        lower_bf = sb("lower_bf", [P, P], BF16)
        ones_bf = sb("ones_bf", [P, P], BF16)
        ones_col = sb("ones_col", [P, 1])
        sel = sb("sel", [P, NJ, P], F32R)
        head_mask = sb("head_mask", [P, NJ, H])
        iota_e = sb("iota_e", [P, T, E])
        step128 = sb("step128", [P, E, T])
        before = sb("before", [P, E, E])
        iota_s = sb("iota_s", [P, S, E])
        neg_half = sb("neg_half", [P, T])
        nothing = sb("nothing", [P, 1])

        wqk_hi = sb("wqk_hi", [P, 2, INNER], F32R)
        wqk_lo = sb("wqk_lo", [P, 2, INNER], F32R)
        vo = sb("vo", [P, H, P])
        wgu_hi = sb("wgu_hi", [P, E * 2 * F], F32R)
        wgu_lo = sb("wgu_lo", [P, E * 2 * F], F32R)
        wd = sb("wd", [P, E * 2 * P])
        wr_t = sb("wr_t", [P, E])
        bf_col = sb("bf_col", [P, 1])
        bf_row = sb("bf_row", [P, D])
        gamma_row = sb("gamma_row", [P, P])
        beta_row = sb("beta_row", [P, P])
        mod = sb("mod", [P, B * 6 * P])
        bout_col = sb("bout_col", [P, 1])
        ga_col = sb("ga_col", [P, B, 2])

        q_act = sb("q_act", [P, G, NJ, 4 * P])
        flat = q_act[:, :, :, :].rearrange("p g j n -> p (g j n)")
        wqkv_nat = flat[:, 0:3 * INNER]
        wg_nat = flat[:, 3072:5120].rearrange("p (k c) -> p k c", c=P)
        wu_nat = flat[:, 5120:7168].rearrange("p (k c) -> p k c", c=P)
        hs = sb("hs", [P, S, P])
        y_sb = hs
        arena_k = sb("arena_k", [P, 3 * INNER])
        arena_x = sb("arena_x", [P, 2 * INNER])
        arena_a = sb("arena_a", [P, 2 * INNER])
        arena_t = sb("arena_t", [P, 2 * INNER])
        wd_nat = arena_a[:, :].rearrange("p (e f) -> p e f", e=E)
        wt = arena_k[:, :].rearrange("p (k c) -> p k c", c=P)
        wo_bd = arena_x[:, :].rearrange("p (j c) -> p j c", c=2 * P)
        sel_f = arena_t[:, 0:INNER].rearrange("p (j c) -> p j c", c=P)
        wmod_sb = arena_t[:, INNER:INNER + 6 * P]
        c_t = sb("c_t", [P, B])

        x_sb = arena_x[:, 0:INNER].rearrange("p (t c) -> p t c", c=P)
        h_sb = arena_x[:, INNER:2 * INNER].rearrange("p (t c) -> p t c", c=P)
        ht_hi = sb("ht_hi", [P, T * P], F32R)
        ht_lo = sb("ht_lo", [P, T * P], F32R)
        kf = arena_k[:, 0:2 * INNER].rearrange("p (a n) -> p a n", a=2)
        k_sum = arena_k[:, 2 * INNER:3 * INNER]
        gt_sb = sb("gt_sb", [P, INNER])
        ks_bd = sb("ks_bd", [P, NJ, H])
        m_sb = sb("m_sb", [P, NJ, P])
        norm_sb = sb("norm_sb", [H, 4 * P])
        recip_in = sb("recip_in", [P, 4, H])
        recip = sb("recip", [P, 4, 2 * 32])
        r_parts = sb("r_parts", [P, G, 4 * P], F32R)
        c_b = gt_sb[:, 0:B * P].rearrange("p (b c) -> p b c", c=P)
        qn = arena_a[:, 0:INNER].rearrange("p (a n) -> p a n", a=2)
        at_sb = arena_a[:, INNER:2 * INNER].rearrange("p (a n) -> p a n", a=2)
        ga_now = sb("ga_now", [P, 2])
        h2 = arena_t[:, 0:INNER].rearrange("p (t c) -> p t c", c=P)
        x2 = arena_t[:, INNER:2 * INNER].rearrange("p (t c) -> p t c", c=P)
        h2t = flat[:, 0:T * P]
        norm_of = {}
        for k in (1, 2, 3):
            norm_of[k] = (sb(f"stats{k}", [P, T, 6]), sb(f"mv{k}", [P, T, 2]), sb(f"var_e{k}", [P, T]),
                          sb(f"rstd{k}", [P, T]))
        logit = sb("logit", [P, T, E])
        code = sb("code", [P, T, E])
        eq = sb("eq", [P, T, E])
        pick1 = sb("pick1", [P, T, E])
        pick2 = sb("pick2", [P, T, E])
        picks_bf = sb("picks_bf", [P, 2 * T - 1, E], BF16)
        top1 = sb("top1", [P, T])
        top2 = sb("top2", [P, T])
        first = sb("first", [P, T])
        gap = sb("gap", [P, T])
        th = sb("th", [P, T])
        w1 = sb("w1", [P, T])
        w2 = sb("w2", [P, T])
        over = sb("over", [P, E, T])
        n_tiles = sb("n_tiles", [P, E])
        prior = sb("prior", [P, E, E])
        tile0 = sb("tile0", [P, E])
        tile1 = sb("tile1", [P, E])
        passed = sb("passed", [P, S, E])
        owner = sb("owner", [P, S])
        owner_i = sb("owner_i", [P, S], U32)
        slot = sb("slot", [P, T, E])
        slot_p = sb("slot_p", [P, T, E])
        slots = sb("slots", [P, 2 * T])
        slots_i = sb("slots_i", [P, 2 * T], U32)
        hst_hi = sb("hst_hi", [P, 2, 4 * P], F32R)
        hst_lo = sb("hst_lo", [P, 2, 4 * P], F32R)
        gate = sb("gate", [P, 2, F])
        hid = sb("hid", [P, 2, F])
        hid_t = sb("hid_t", [P, 2, F])
        wf_bd = hid[:, 0, 0:P]
        wr_nat = hid[0:E, 1, 0:P]
        c_nat = hid[0:B, 1, P:2 * P]
        sign_b = gate[:, :, :].rearrange("p a (b c) -> p (a b) c", c=P)
        y1 = kf[:, 0, :].rearrange("p (t c) -> p t c", c=P)
        y2 = kf[:, 1, :].rearrange("p (t c) -> p t c", c=P)
        res = h2

        bank = [ctx.enter_context(nc.psum_tensor(f"bank{i}", [P, 512], F32)) for i in range(8)]

        rows_in = nc.dram_tensor("rows_in", [S * P, P], F32, kind="Internal").ap()
        rows_out = nc.dram_tensor("rows_out", [S * P, P], F32, kind="Internal").ap()

        const_ready = sem("const_ready")
        zeroed = sem("zeroed")
        in_qkv, in_heads, in_gu, in_down, in_cond, in_rows = (
            sem(n) for n in ("in_qkv", "in_heads", "in_gu", "in_down", "in_cond", "in_rows"))
        su_full, su_act, su_dve = sem("su_full"), sem("su_act"), sem("su_dve")
        sel_ready, c_wide = sem("sel_ready"), sem("c_wide")
        held = sem("held")
        pool_chain = sem("pool_chain")
        dve_chain = sem("dve_chain")
        act_chain = sem("act_chain")
        names = """x_in x_used var1 rstd1 var2 rstd2 var3 rstd3 h_ready ht_full ht_act ht_dve k_full k_biased k_relu
            g_done k_added q_full q_ready gt_copied ksum_full ks_ready m_full m_copied norm_full norm_copied normt_full
            r_ready rt_full r_hi r_lo rb_full qn_ready out_done at_copied att_full ga_ready x2_ready h2_ready h2t_full
            h2t_copied logit_full gap_ready tanh_done picks_ready rank_full owner_ready route_ready scattered ft_full
            ft_hi ft_lo gu_full silu_done hid_ready hidt_full hidt_copied y_full y_copied y_stored gathered res_ready
            stored""".split()
        sm = {n: sem(n) for n in names}
        hs_in = [sem(f"hs_in{q}") for q in range(NQ)]

        Z = (0, 1, 4)
        MB = (6, 7, 2, 3)
        FT, HT, YB = (2, 4), (3, 6), (5, 7)
        SETUP_JOBS = 2 + 6 + 2 * B + 4 + 4 + E + 4

        def quad(q):
            return range(4 * q, min(4 * q + 4, S))

        block = ctx.enter_context(nc.Block())

        @block.sync
        def _(sp):
            sp.dma_start(wqkv_nat, wqkv).then_inc(in_qkv, 16)
            sp.wait_ge(zeroed, 2)
            for s in range(2):
                lo, hi = s * D, (s + 1) * D
                sp.dma_start(wf_bd[lo:hi, lo:hi], wf).then_inc(in_heads, 16)
                sp.dma_start(wo_bd[lo:hi, :, s * P:(s + 1) * P],
                             wout.rearrange("(j s e) d -> s e j d", s=2, e=D)[s]).then_inc(in_heads, 16)
                sp.dma_start(bf_col[lo:hi, :], bf.rearrange("(e a) -> e a", a=1)).then_inc(in_rows, 16)
            sp.dma_start(wg_nat, wgate.rearrange("e (k p) c -> p (e k) c", p=P)).then_inc(in_gu, 16)
            sp.dma_start(wu_nat, wup.rearrange("e (k p) c -> p (e k) c", p=P)).then_inc(in_gu, 16)
            sp.dma_start(wd_nat, wdown.rearrange("e d f -> d e f")).then_inc(in_down, 16)
            for row, src in ((bf_row, bf), (gamma_row, gamma), (beta_row, beta)):
                sp.dma_start(row[:, :], src.partition_broadcast(P)).then_inc(in_rows, 16)
            sp.dma_start(bout_col[:, :], bout.rearrange("(e a) -> e a", a=1)).then_inc(in_rows, 16)
            sp.wait_ge(zeroed, 3)
            sp.dma_start(rows_in.rearrange("(s p) c -> p s c", p=P), hs[:, :, :]).then_inc(sm["stored"], 16)

            def load_x(b):
                at = bass.ds(b * (N * C), N * C)
                sp.dma_start(x_sb[:, :, :], x_flat[at].rearrange("(t p c) -> p t c", p=P, c=C)
                             ).then_inc(sm["x_in"], 16)

            def move_rows(b):
                sp.wait_ge(sm["scattered"], b * (32 * T) + 32 * T)
                for q in range(NQ):
                    n = len(quad(q))
                    sp.dma_start(hs[:, 4 * q:4 * q + n, :],
                                 rows_in[4 * q * P:(4 * q + n) * P, :].rearrange("(s p) c -> p s c", p=P)
                                 ).then_inc(hs_in[q], 16)
                for q in range(NQ):
                    n = len(quad(q))
                    sp.wait_ge(sm["y_copied"], b * S + 4 * q + n)
                    sp.dma_start(rows_out[4 * q * P:(4 * q + n) * P, :].rearrange("(s p) c -> p s c", p=P),
                                 y_sb[:, 4 * q:4 * q + n, :]).then_inc(sm["y_stored"], 16)

            def store(b):
                at = bass.ds(b * (N * C), N * C)
                sp.wait_ge(sm["res_ready"], b + 1)
                sp.dma_start(out_flat[at].rearrange("(t p c) -> p t c", p=P, c=C), res[:, :, :]
                             ).then_inc(sm["stored"], 16)

            def batch(b, prev, last=False):
                if not last:
                    if prev is not None:
                        sp.wait_ge(sm["x2_ready"], prev * G + G)
                    else:
                        sp.wait_ge(sm["x_used"], 1)
                    load_x(b + 1)
                if prev is not None:
                    move_rows(prev)
                if last:
                    sp.wait_ge(sm["x2_ready"], prev * G + G)
                else:
                    sp.wait_ge(sm["x_used"], b + 2)
                load_x(b)
                if prev is not None:
                    store(prev)

            x_flat, out_flat = x.rearrange("b n c -> (b n c)"), out.rearrange("b n c -> (b n c)")
            sp.wait_ge(su_act, SETUP_JOBS)
            load_x(0)
            batch(0, None)
            with sp.Fori(1, B - 1) as b:
                batch(b, b - 1)
            batch(B - 1, B - 2, last=True)
            move_rows(B - 1)
            store(B - 1)
            sp.wait_ge(sm["stored"], 16 * B + 16)

        @block.gpsimd
        def _(pool):
            n = [0]

            def link(ins):
                n[0] += 1
                ins.then_inc(pool_chain, 1)
                pool.wait_ge(pool_chain, n[0])

            pool.memset(neg_half[:, :], -0.5)
            pool.memset(nothing[:, :], 0.0)
            pool.memset(wf_bd[:, :], 0.0).then_inc(zeroed, 1)
            pool.memset(wo_bd[:, :, :], 0.0).then_inc(zeroed, 1)
            pool.memset(hs[:, :, :], 0.0).then_inc(zeroed, 1)
            pool.memset(ident[:, :], 0.0)
            pool.memset(lower_bf[:, :], 1.0)
            pool.memset(ones_bf[:, :], 1.0)
            pool.memset(ones_col[:, :], 1.0)
            pool.memset(sel_f[:, :, :], 0.0)
            pool.memset(head_mask[:, :, :], 0.0)
            pool.memset(before[:, :, :], 1.0)
            link(pool.memset(iota_e[:, :, :], 0.0))

            def select(ap, compare, fill, base, pattern, per_row):
                link(pool.affine_select(out=ap, in_=ap, compare_op=compare, fill=fill, base=base,
                                        pattern=pattern, channel_multiplier=per_row))
            select(ident[:, :], ALU.not_equal, 1.0, 0, [[-1, P]], 1)
            select(lower_bf[:, :], ALU.is_gt, 0.0, 0, [[1, P]], -1)
            sel_v = sel_f[:, :, :].rearrange("p j (s e) -> p j s e", s=2)
            for base in (0, -32):
                select(sel_v, ALU.not_equal, 1.0, base, [[-2, NJ], [-1, 2], [0, D]], 1)
            for s in range(2):
                select(head_mask[s * D:(s + 1) * D, :, :], ALU.not_equal, 1.0, -s, [[-2, NJ], [1, H]], 0)
            select(before[:, :, :], ALU.is_gt, 0.0, 0, [[1, E], [-1, E]], 0)
            pool.iota(iota_e[:, :, :], [[0, T], [1, E]], base=0, channel_multiplier=0,
                      allow_small_or_imprecise_dtypes=True)
            pool.iota(step128[:, :, :], [[0, E], [P, T]], base=0, channel_multiplier=0,
                      allow_small_or_imprecise_dtypes=True)
            link(pool.iota(iota_s[:, :, :], [[1, S], [0, E]], base=0, channel_multiplier=0,
                           allow_small_or_imprecise_dtypes=True))
            pool.memset(ones_col[:, :], 1.0).then_inc(const_ready, 1)
            pool.wait_ge(sm["stored"], 16)

            def rsqrt(k, b):
                _, _, var_e, rstd = norm_of[k]
                pool.wait_ge(sm[f"var{k}"], b + 1)
                pool.tensor_tensor(rstd[:, :], var_e[:, :], neg_half[:, :], ALU.pow).then_inc(sm[f"rstd{k}"], 1)

            def hold(name, value):
                pool.wait_ge(sm[name], value)
                pool.tensor_tensor(nothing[:, :], nothing[:, :], nothing[:, :], ALU.add).then_inc(held, 1)

            def sum_keys(b, prev):
                for t in range(1, T):
                    if t == 2 and prev is not None:
                        rsqrt(2, prev)
                    pool.wait_ge(sm["k_relu"], b * 2 * T + 2 * t + 2)
                    if t >= 2:
                        pool.wait_ge(sm["k_added"], b * (T - 1) + t - 1)
                    pool.tensor_tensor(k_sum[:, :], kf[:, 0, :] if t == 1 else k_sum[:, :], kf[:, t % 2, :],
                                       ALU.add).then_inc(sm["k_added"], 1)

            def scatter(b):
                hold("route_ready", b + 1)
                for t in range(T):
                    for k in range(2):
                        pool.indirect_dma_start(
                            out=rows_in, out_offset=bass.IndirectOffsetOnAxis(slots_i[:, k * T + t:k * T + t + 1], 0),
                            in_=h2[:, t, :], in_offset=None).then_inc(sm["scattered"], 16)

            def gather(b):
                pool.wait_ge(held, b * 2 + 1)
                hold("y_stored", b * (16 * NQ) + 16 * NQ)
                for t in range(T):
                    for k, y in enumerate((y1, y2)):
                        pool.indirect_dma_start(
                            out=y[:, t, :], out_offset=None, in_=rows_out,
                            in_offset=bass.IndirectOffsetOnAxis(slots_i[:, k * T + t:k * T + t + 1], 0),
                        ).then_inc(sm["gathered"], 16)
                pool.wait_ge(held, b * 2 + 2)
                rsqrt(3, b)

            def batch(b, prev, last=False):
                sum_keys(b, prev)
                if prev is not None:
                    scatter(prev)
                if not last:
                    rsqrt(1, b + 1)
                if prev is not None:
                    gather(prev)

            rsqrt(1, 0)
            batch(0, None)
            with pool.Fori(1, B - 1) as b:
                batch(b, b - 1)
            batch(B - 1, B - 2, last=True)
            rsqrt(2, B - 1)
            scatter(B - 1)
            gather(B - 1)

        @block.scalar
        def _(act):
            act.dma_start(c_nat[:, :], cond).then_inc(in_cond, 16)
            act.dma_start(wmod_sb[:, :], wmod).then_inc(in_cond, 16)
            act.dma_start(wr_nat[:, :], wrouter).then_inc(in_cond, 16)
            job = [0]

            def evac(dst):
                act.wait_ge(su_full, job[0] + 1)
                src = bank[job[0] % 8][:, 0:512]
                act.activation(dst, src, ACT.Copy).then_inc(su_act, 1)
                job[0] += 1

            act.wait_ge(su_full, 1)
            act.activation(wr_t[:, :], bank[0][:, 0:E], ACT.Copy)
            act.activation(c_t[:, :], bank[0][:, 16:16 + B], ACT.Silu).then_inc(su_act, 1)
            act.wait_ge(su_act, 1)
            for b in range(B):
                act.activation(c_b[:, b, :], c_t[:, b:b + 1].to_broadcast([P, P]), ACT.Copy).then_inc(c_wide, 1)
            job[0] = 1
            act.wait_ge(su_full, 2)
            act.activation(ga_col[:, :, 0], bank[1][:, 0:B], ACT.Copy).then_inc(su_act, 1)
            job[0] = 2
            for k in range(6):
                evac(wt[:, 4 * k:4 * k + 4, :])
            for k in range(2 * B):
                half = mod[:, (k // 2) * 768 + (k % 2) * 384:(k // 2) * 768 + (k % 2) * 384 + 384]
                act.wait_ge(su_full, job[0] + 1)
                act.activation(half, bank[job[0] % 8][:, 0:384], ACT.Copy).then_inc(su_act, 1)
                job[0] += 1
            for k in range(4):
                evac(wqk_hi[:, k // 2, (k % 2) * 512:(k % 2) * 512 + 512])
            for k in range(4):
                evac(vo[:, 4 * k:4 * k + 4, :])
            for e in range(E):
                evac(wgu_hi[:, e * 512:e * 512 + 512])
            for k in range(4):
                evac(wd[:, k * 512:k * 512 + 512])

            def transposed(b):
                for g in range(G):
                    act.wait_ge(sm["ht_full"], b * G + g + 1)
                    act.activation(ht_hi[:, g * 512:g * 512 + 512], bank[g][:, :], ACT.Copy).then_inc(sm["ht_act"], 1)

            def keys(b, prev):
                for i in range(2 * T):
                    act.wait_ge(sm["k_biased"], b * 2 * T + i + 1)
                    half = kf[:, (i // 2) % 2, (i % 2) * 512:(i % 2) * 512 + 512]
                    act.activation(half, half, ACT.Relu).then_inc(sm["k_relu"], 1)
                    if prev is not None and i == 2 * 4 + 1:
                        for g in range(G):
                            act.wait_ge(sm["h2t_full"], prev * G + g + 1)
                            act.activation(h2t[:, g * 512:g * 512 + 512], bank[6 + g][:, :], ACT.Copy
                                           ).then_inc(sm["h2t_copied"], 1)
                    if prev is not None and i == 2 * 6 + 1:
                        gap_tanh(prev)

            def gap_tanh(b):
                act.wait_ge(sm["gap_ready"], b + 1)
                act.activation(th[:, :], gap[:, :], ACT.Tanh, scale=0.5).then_inc(sm["tanh_done"], 1)

            def q_relu(b, g):
                for j in range(NJ):
                    i = NJ * g + j
                    act.wait_ge(sm["q_full"], b * G * NJ + i + 1)
                    act.activation(q_act[:, g, j, :], bank[Z[i % 3]][:, :], ACT.Relu, bias=bf_col[:, 0:1]
                                   ).then_inc(sm["q_ready"], 1)

            def norms(b, g):
                act.wait_ge(sm["norm_full"], b * G + g + 1)
                act.activation(norm_sb[:, :], bank[5][0:H, :], ACT.Copy).then_inc(sm["norm_copied"], 1)

            def recips(b, g):
                act.wait_ge(sm["rt_full"], b * G + g + 1)
                act.activation(r_parts[0:64, g, :], bank[6 + g][0:64, :], ACT.Copy).then_inc(sm["r_hi"], 1)

            def queries(b):
                act.wait_ge(sm["g_done"], b * T + T)
                for k in range(2):
                    act.activation(gt_sb[:, k * 512:k * 512 + 512], bank[2 + k][:, :], ACT.Copy
                                   ).then_inc(sm["gt_copied"], 1)
                q_relu(b, 0)
                for k in range(4):
                    act.wait_ge(sm["m_full"], b * 4 + k + 1)
                    mb = bank[MB[k]][:, :].rearrange("p (a s d) -> p a s d", a=2, s=2)
                    act.activation(m_sb[0:D, 2 * k:2 * k + 2, :], mb[0:D, :, 0, :], ACT.Copy)
                    act.activation(m_sb[D:P, 2 * k:2 * k + 2, :], mb[D:P, :, 1, :], ACT.Copy
                                   ).then_inc(sm["m_copied"], 1)
                q_relu(b, 1)
                norms(b, 0)
                norms(b, 1)
                recips(b, 0)

            def experts(b):
                def fhi(q):
                    w = len(quad(q)) * P
                    act.wait_ge(sm["ft_full"], b * NQ + q + 1)
                    if q >= 2:
                        act.wait_ge(sm["gu_full"], b * S + 4 * q - 4)
                    act.activation(hst_hi[:, q % 2, 0:w], bank[FT[q % 2]][:, 0:w], ACT.Copy).then_inc(sm["ft_hi"], 1)

                fhi(0)
                for i in range(S + 1):
                    if i < S:
                        if i % 4 == 0 and i // 4 + 1 < NQ:
                            fhi(i // 4 + 1)
                        act.wait_ge(sm["gu_full"], b * S + i + 1)
                        if i >= 2:
                            act.wait_ge(sm["hid_ready"], b * S + i - 1)
                        act.activation(gate[:, i % 2, :], bank[i % 2][:, 0:F], ACT.Silu).then_inc(sm["silu_done"], 1)
                    if i >= 1:
                        act.wait_ge(sm["hidt_full"], b * S + i)
                        if i >= 3:
                            act.wait_ge(sm["y_full"], b * S + i - 2)
                        act.activation(hid_t[:, (i - 1) % 2, :], bank[HT[(i - 1) % 2]][:, 0:F], ACT.Copy
                                       ).then_inc(sm["hidt_copied"], 1)

            def attended(b, last):
                if not last:
                    transposed(b + 1)
                for g in range(G):
                    if g:
                        recips(b, 1)
                    act.wait_ge(sm["out_done"], b * G * NJ + NJ * (g + 1))
                    act.activation(at_sb[:, g, :], bank[4 + g][:, :], ACT.Identity, scale=ga_now[:, 0:1],
                                   bias=ga_now[:, 1:2]).then_inc(sm["at_copied"], 1)

            def batch(b, prev, last=False):
                keys(b, prev)
                queries(b)
                if prev is not None:
                    experts(prev)
                attended(b, last)

            transposed(0)
            batch(0, None)
            with act.Fori(1, B - 1) as b:
                batch(b, b - 1)
            batch(B - 1, B - 2, last=True)
            for g in range(G):
                act.wait_ge(sm["h2t_full"], (B - 1) * G + g + 1)
                act.activation(h2t[:, g * 512:g * 512 + 512], bank[6 + g][:, :], ACT.Copy).then_inc(sm["h2t_copied"], 1)
            gap_tanh(B - 1)
            experts(B - 1)

        @block.vector
        def _(dve):
            n = [0]

            def link(ins):
                n[0] += 1
                ins.then_inc(dve_chain, 1)
                dve.wait_ge(dve_chain, n[0])

            def rows(ap2d, k=T):
                return ap2d.unsqueeze(1).to_broadcast([P, k, P])

            dve.wait_ge(const_ready, 1)
            dve.tensor_copy(sel[:, :, :], sel_f[:, :, :]).then_inc(sel_ready, 1)
            dve.wait_ge(in_rows, 16 * 6)
            dve.wait_ge(su_act, 2 + 6 + 2 * B)
            mod_v = mod[:, :].rearrange("p (b k c) -> p b k c", b=B, k=6)

            def gate_of(v, sign):
                link(dve.tensor_scalar(sign, v, 0.0, 2.0, ALU.is_ge, ALU.mult))
                link(dve.tensor_scalar(sign, sign, -1.0, None, ALU.add))
                link(dve.tensor_tensor(v, v, sign, ALU.mult))
                link(dve.scalar_tensor_tensor(v, v, 0.25, sign, ALU.max, ALU.mult))

            for k in (1, 4):
                dve.tensor_scalar(mod_v[:, :, k, :], mod_v[:, :, k, :], 1.0, None, ALU.add)
            gate_of(mod_v[:, :, 5, :], sign_b)
            gate_of(ga_col[:, :, 0], th[:, 0:B])
            link(dve.tensor_tensor(mod_v[:, :, 2, :], mod_v[:, :, 5, :], rows(gamma_row[:, :], B), ALU.mult))
            dve.tensor_tensor(mod_v[:, :, 5, :], mod_v[:, :, 5, :], rows(beta_row[:, :], B), ALU.mult)
            link(dve.tensor_scalar(ga_col[:, :, 1], ga_col[:, :, 0], bout_col[:, 0:1], None, ALU.mult))

            def rest(j, dst, hi):
                dve.wait_ge(su_act, j + 1)
                dve.tensor_tensor(dst, bank[j % 8][:, :], hi.bitcast(F32), ALU.subtract).then_inc(su_dve, 1)

            j0 = 2 + 6 + 2 * B
            for k in range(4):
                o = (k % 2) * 512
                rest(j0 + k, wqk_lo[:, k // 2, o:o + 512], wqk_hi[:, k // 2, o:o + 512])
            for e in range(E):
                rest(j0 + 8 + e, wgu_lo[:, e * 512:e * 512 + 512], wgu_hi[:, e * 512:e * 512 + 512])
            dve.memset(picks_bf[:, :, :], 0.0)
            dve.memset(r_parts[:, :, :].bitcast(F32), 0.0)
            link(dve.memset(recip[:, :, :], 0.0))

            def modrow(b, k):
                return rows(mod[:, bass.ds(b * (6 * P) + k * P, P)])

            def statistics(k, src):
                stats, mv, var_e, _ = norm_of[k]
                for t in range(T):
                    ins = dve.bn_stats(stats[:, t, :], src[:, t, :])
                link(ins)
                for t in range(T):
                    ins = dve.bn_aggr(mv[:, t, :], stats[:, t, :])
                link(ins)
                dve.tensor_scalar(var_e[:, :], mv[:, :, 1], EPS, None, ALU.add).then_inc(sm[f"var{k}"], 1)

            def normalise(k, b, dst, src):
                _, mv, _, rstd = norm_of[k]
                dve.wait_ge(sm[f"rstd{k}"], b + 1)
                for t in range(T):
                    ins = dve.tensor_scalar(dst[:, t, :], src[:, t, :], mv[:, t, 0:1], rstd[:, t:t + 1],
                                            ALU.subtract, ALU.mult)
                return ins

            def norm1(b):
                dve.wait_ge(sm["x_in"], x_loads(b))
                statistics(1, x_sb)
                normalise(1, b, h_sb, x_sb).then_inc(sm["x_used"], 1)
                dve.wait_ge(sm["x_used"], b + 1)
                link(dve.tensor_tensor(h_sb[:, :, :], h_sb[:, :, :], modrow(b, 1), ALU.mult))
                dve.tensor_tensor(h_sb[:, :, :], h_sb[:, :, :], modrow(b, 0), ALU.add).then_inc(sm["h_ready"], 1)

            def x_loads(b):
                return 16 if isinstance(b, int) and b == 0 else b * 32

            def h_rest(b):
                for g in range(G):
                    dve.wait_ge(sm["ht_act"], b * G + g + 1)
                    o = g * 512
                    dve.tensor_tensor(ht_lo[:, o:o + 512], bank[g][:, :], ht_hi[:, o:o + 512].bitcast(F32),
                                      ALU.subtract).then_inc(sm["ht_dve"], 1)

            def wide(ap, k=E):
                return ap.unsqueeze(2).to_broadcast([P, ap.shape[1], k])

            def picks(b):
                dve.wait_ge(sm["logit_full"], b + 1)
                link(dve.tensor_copy(logit[:, :, :], bank[5][:, 0:T * E].rearrange("p (t e) -> p t e", e=E)))
                for top, pick in ((top1, pick1), (top2, pick2)):
                    link(dve.tensor_reduce(top[:, :], logit[:, :, :], AX_X, ALU.max))
                    link(dve.tensor_tensor(eq[:, :, :], logit[:, :, :], wide(top[:, :]), ALU.is_equal))
                    link(dve.scalar_tensor_tensor(code[:, :, :], eq[:, :, :], -float(E), iota_e[:, :, :],
                                                  ALU.mult, ALU.add))
                    link(dve.tensor_reduce(first[:, :], code[:, :, :], AX_X, ALU.min))
                    link(dve.tensor_tensor(pick[:, :, :], code[:, :, :], wide(first[:, :]), ALU.is_equal))
                    if top is top1:
                        link(dve.scalar_tensor_tensor(logit[:, :, :], pick[:, :, :], -BIG, logit[:, :, :],
                                                      ALU.mult, ALU.add))
                dve.tensor_tensor(picks_bf[:, T - 1:, :], pick1[:, :, :], pick2[:, :, :], ALU.add
                                  ).then_inc(sm["picks_ready"], 1)
                dve.tensor_tensor(gap[:, :], top2[:, :], top1[:, :], ALU.subtract).then_inc(sm["gap_ready"], 1)

            def route(b):
                dve.wait_ge(sm["rank_full"], b + 1)
                count = bank[6][:, 0:E].unsqueeze(2).to_broadcast([P, E, T])
                link(dve.tensor_tensor(over[:, :, :], count, step128[:, :, :], ALU.is_gt))
                link(dve.tensor_reduce(n_tiles[:, :], over[:, :, :], AX_X, ALU.add))
                link(dve.tensor_tensor(prior[:, :, :], before[:, :, :],
                                       n_tiles[:, :].unsqueeze(1).to_broadcast([P, E, E]), ALU.mult))
                link(dve.tensor_reduce(tile0[:, :], prior[:, :, :], AX_X, ALU.add))
                link(dve.scalar_tensor_tensor(slot[:, :, :], tile0[:, :].unsqueeze(1).to_broadcast([P, T, E]),
                                              float(P), bank[5][:, 64:128].rearrange("p (t e) -> p t e", e=E),
                                              ALU.mult, ALU.add))
                for k, pick in enumerate((pick1, pick2)):
                    link(dve.tensor_tensor(slot_p[:, :, :], slot[:, :, :], pick[:, :, :], ALU.mult))
                    link(dve.tensor_reduce(slots[:, k * T:(k + 1) * T], slot_p[:, :, :], AX_X, ALU.add))
                dve.tensor_copy(slots_i[:, :], slots[:, :]).then_inc(sm["route_ready"], 1)
                link(dve.tensor_tensor(tile1[:, :], tile0[:, :], n_tiles[:, :], ALU.add))
                link(dve.tensor_tensor(passed[:, :, :], tile1[:, :].unsqueeze(1).to_broadcast([P, S, E]),
                                       iota_s[:, :, :], ALU.is_le))
                link(dve.tensor_reduce(owner[:, :], passed[:, :, :], AX_X, ALU.add))
                dve.tensor_scalar(owner_i[:, :], owner[:, :], float(E - 1), None, ALU.min
                                  ).then_inc(sm["owner_ready"], 1)
                dve.wait_ge(sm["tanh_done"], b + 1)
                dve.tensor_scalar(w2[:, :], th[:, :], 0.5, 0.5, ALU.mult, ALU.add)
                link(dve.tensor_scalar(w1[:, :], th[:, :], -0.5, 0.5, ALU.mult, ALU.add))

            def norm2(b, part):
                if part == 0:
                    dve.wait_ge(sm["x2_ready"], b * G + G)
                    statistics(2, x2)
                else:
                    link(normalise(2, b, h2, x2))
                    link(dve.tensor_tensor(h2[:, :, :], h2[:, :, :], modrow(b, 4), ALU.mult))
                    dve.tensor_tensor(h2[:, :, :], h2[:, :, :], modrow(b, 3), ALU.add).then_inc(sm["h2_ready"], 1)

            def keys(b, prev):
                bias = bf_row[:, :].unsqueeze(1).to_broadcast([P, 512 // D, D])
                for i in range(2 * T):
                    t = i // 2
                    dve.wait_ge(sm["k_full"], b * 2 * T + i + 1)
                    if i % 2 == 0 and t >= 2:
                        dve.wait_ge(sm["g_done"], b * T + t - 1)
                        dve.wait_ge(sm["k_added"], b * (T - 1) + max(1, t - 2))
                    dst = kf[:, t % 2, (i % 2) * 512:(i % 2) * 512 + 512]
                    dve.tensor_tensor(dst.rearrange("p (h d) -> p h d", d=D),
                                      bank[Z[i % 3]][:, :].rearrange("p (h d) -> p h d", d=D), bias, ALU.add
                                      ).then_inc(sm["k_biased"], 1)
                    if prev is not None and i % 2:
                        if t == 0:
                            norm2(prev, 0)
                        elif t == 2:
                            dve.wait_ge(sm["stored"], prev * 16 + 16)
                            norm2(prev, 1)
                        elif t == 5:
                            picks(prev)
                        elif t == T - 1:
                            route(prev)

            def queries(b):
                link(dve.tensor_copy(ga_now[:, :], ga_col[:, :, :].rearrange("p b k -> p (b k)")[:, bass.ds(b * 2, 2)]))
                dve.wait_ge(sm["ksum_full"], b + 1)
                dve.tensor_tensor(ks_bd[:, :, :], head_mask[:, :, :],
                                  bank[5][:, 0:NJ].unsqueeze(2).to_broadcast([P, NJ, H]), ALU.mult
                                  ).then_inc(sm["ks_ready"], 1)
                recips(b, 0)

            def recips(b, g):
                dve.wait_ge(sm["normt_full"], b * G + g + 1)
                link(dve.tensor_scalar(recip_in[:, :, :],
                                       bank[6 + g][:, 0:4 * H].rearrange("p (t h) -> p t h", h=H),
                                       1e-6, None, ALU.add))
                link(dve.reciprocal(recip[:, :, 0:H], recip_in[:, :, :]))
                dve.tensor_copy(recip[:, :, 32:32 + H], recip[:, :, 0:H]).then_inc(sm["r_ready"], 1)

            def recips_rest(b, g):
                dve.wait_ge(sm["r_hi"], b * G + g + 1)
                dve.tensor_tensor(r_parts[32:64, g, :], bank[6 + g][32:64, :], r_parts[32:64, g, :].bitcast(F32),
                                  ALU.subtract).then_inc(sm["r_lo"], 1)

            def experts(b):
                def flo(q):
                    w = len(quad(q)) * P
                    dve.wait_ge(sm["ft_hi"], b * NQ + q + 1)
                    dve.tensor_tensor(hst_lo[:, q % 2, 0:w], bank[FT[q % 2]][:, 0:w],
                                      hst_hi[:, q % 2, 0:w].bitcast(F32), ALU.subtract).then_inc(sm["ft_lo"], 1)

                flo(0)
                for i in range(S + 2):
                    if i < S:
                        if i % 4 == 0 and i // 4 + 1 < NQ:
                            flo(i // 4 + 1)
                        dve.wait_ge(sm["silu_done"], b * S + i + 1)
                        if i >= 2:
                            dve.wait_ge(sm["hidt_full"], b * S + i - 1)
                        dve.tensor_tensor(hid[:, i % 2, :], bank[i % 2][:, F:2 * F], gate[:, i % 2, :], ALU.mult
                                          ).then_inc(sm["hid_ready"], 1)
                    if i >= 2:
                        dve.wait_ge(sm["y_full"], b * S + i - 1)
                        dve.tensor_copy(y_sb[:, i - 2, :], bank[YB[i % 2]][:, 0:P]).then_inc(sm["y_copied"], 1)

            def combine(b):
                dve.wait_ge(sm["gathered"], b * (32 * T) + 32 * T)
                for t in range(T):
                    ins = dve.tensor_scalar(y1[:, t, :], y1[:, t, :], w1[:, t:t + 1], None, ALU.mult)
                link(ins)
                for t in range(T):
                    ins = dve.scalar_tensor_tensor(y1[:, t, :], y2[:, t, :], w2[:, t:t + 1], y1[:, t, :],
                                                   ALU.mult, ALU.add)
                link(ins)
                statistics(3, y1)
                link(normalise(3, b, y1, y1))
                link(dve.tensor_tensor(y1[:, :, :], y1[:, :, :], modrow(b, 2), ALU.mult))
                link(dve.tensor_tensor(y1[:, :, :], y1[:, :, :], modrow(b, 5), ALU.add))
                dve.tensor_tensor(res[:, :, :], y1[:, :, :], x2[:, :, :], ALU.add).then_inc(sm["res_ready"], 1)

            def attended(b, prev, last):
                if not last:
                    h_rest(b + 1)
                for g in range(G):
                    if g:
                        recips_rest(b, 1)
                    for j in range(NJ):
                        i = NJ * g + j
                        dve.wait_ge(sm["rb_full"], b * G * NJ + i + 1)
                        if i >= 2:
                            dve.wait_ge(sm["out_done"], b * G * NJ + i - 1)
                        dve.tensor_tensor(qn[:, i % 2, :], bank[2 + i % 2][:, :], q_act[:, g, j, :], ALU.mult
                                          ).then_inc(sm["qn_ready"], 1)
                if prev is not None:
                    combine(prev)
                    dve.wait_ge(sm["res_ready"], prev + 1)
                dve.wait_ge(sm["x_in"], 32 * B if last else b * 32 + 48)
                for g in range(G):
                    dve.wait_ge(sm["att_full"], b * G + g + 1)
                    dve.tensor_tensor(x2[:, 4 * g:4 * g + 4, :],
                                      bank[6 + g][:, :].rearrange("p (t c) -> p t c", c=P),
                                      x_sb[:, 4 * g:4 * g + 4, :], ALU.add).then_inc(sm["x2_ready"], 1)

            def batch(b, prev, last=False):
                dve.sem_clear(dve_chain)
                n[0] = 0
                keys(b, prev)
                queries(b)
                recips_rest(b, 0)
                recips(b, 1)
                if prev is not None:
                    experts(prev)
                if not last:
                    norm1(b + 1)
                attended(b, prev, last)

            norm1(0)
            h_rest(0)
            batch(0, None)
            with dve.Fori(1, B - 1) as b:
                batch(b, b - 1)
            batch(B - 1, B - 2, last=True)
            dve.sem_clear(dve_chain)
            n[0] = 0
            norm2(B - 1, 0)
            dve.wait_ge(sm["stored"], 16 * B)
            norm2(B - 1, 1)
            picks(B - 1)
            route(B - 1)
            experts(B - 1)
            combine(B - 1)

        @block.tensor
        def _(pe):
            job = [0]
            splits = []

            def take():
                k = job[0] - 8
                if k >= 0:
                    pe.wait_ge(su_act, k + 1)
                    if k in splits:
                        pe.wait_ge(su_dve, splits.index(k) + 1)
                job[0] += 1
                return bank[(job[0] - 1) % 8]

            pe.wait_ge(const_ready, 1)
            pe.wait_ge(in_cond, 48)
            bk = take()
            pe.transpose(bk[:, 0:E], wr_nat[:, :], ident[0:E, 0:E])
            pe.transpose(bk[:, 16:16 + B], c_nat[:, :], ident[0:B, 0:B]).then_inc(su_full, 1)
            pe.wait_ge(su_act, 1)
            bk = take()
            pe.matmul(bk[:, 0:B], wmod_sb[:, 2 * P:3 * P], c_t[:, :], start=True, stop=True).then_inc(su_full, 1)
            pe.wait_ge(in_qkv, 16)
            for k in range(6):
                bk = take()
                for i in range(4):
                    o = (4 * k + i) * P
                    ins = pe.transpose(bk[:, i * P:(i + 1) * P], wqkv_nat[:, o:o + P], ident[:, :])
                ins.then_inc(su_full, 1)
            pe.wait_ge(c_wide, B)
            for k in range(2 * B):
                bk = take()
                o = (k % 2) * 384
                pe.matmul(bk[:, 0:384], c_b[:, k // 2, :], wmod_sb[:, o:o + 384], start=True, stop=True
                          ).then_inc(su_full, 1)
            pe.wait_ge(su_act, 8)
            pe.wait_ge(in_heads, 64)
            for k in range(4):
                splits.append(job[0])
                bk = take()
                for i in range(4):
                    ins = pe.matmul(bk[:, i * P:(i + 1) * P], wt[:, 4 * k + i, :], wf_bd[:, :], start=True, stop=True)
                ins.then_inc(su_full, 1)
            for k in range(4):
                bk = take()
                for i in range(2):
                    j = 2 * k + i
                    ins = pe.matmul(bk[:, i * 256:(i + 1) * 256], wt[:, 16 + j, :], wo_bd[:, j, :],
                                    start=True, stop=True)
                ins.then_inc(su_full, 1)
            pe.wait_ge(in_gu, 32)
            for e in range(E):
                splits.append(job[0])
                bk = take()
                for i in range(4):
                    src = (wg_nat, wu_nat)[i // 2][:, 2 * e + i % 2, :]
                    ins = pe.transpose(bk[:, i * P:(i + 1) * P], src, ident[:, :])
                ins.then_inc(su_full, 1)
            pe.wait_ge(in_down, 16)
            for k in range(4):
                bk = take()
                for i in range(4):
                    e, f = 2 * k + i // 2, i % 2
                    ins = pe.transpose(bk[:, i * P:(i + 1) * P], wd_nat[:, e, f * P:(f + 1) * P], ident[:, :])
                ins.then_inc(su_full, 1)
            pe.wait_ge(su_act, job[0])
            pe.wait_ge(su_dve, 4 + E)
            pe.wait_ge(sel_ready, 1)

            def product(dst, hi, lo, rhs_hi, rhs_lo):
                pe.matmul(dst, hi, rhs_hi, start=True, stop=False)
                pe.matmul(dst, hi, rhs_lo, start=False, stop=False)
                return pe.matmul(dst, lo, rhs_hi, start=False, stop=True)

            def transposes(b, ready, src, full, banks):
                pe.wait_ge(sm[ready], b + 1)
                for g in range(G):
                    for i in range(4):
                        ins = pe.transpose(bank[banks[g]][:, i * P:(i + 1) * P], src[:, 4 * g + i, :], ident[:, :])
                    ins.then_inc(sm[full], 1)

            def keys(b, prev):
                for t in range(T + 1):
                    if t < T:
                        for k in range(2):
                            i = 2 * t + k
                            if i >= 3:
                                pe.wait_ge(sm["k_biased"], b * 2 * T + i - 2)
                            tok, o = slice(t * P, (t + 1) * P), slice(k * 512, k * 512 + 512)
                            product(bank[Z[i % 3]][:, :], ht_hi[:, tok], ht_lo[:, tok], wqk_hi[:, 1, o],
                                    wqk_lo[:, 1, o]).then_inc(sm["k_full"], 1)
                    if prev is not None and t == 4:
                        transposes(prev, "h2_ready", h2, "h2t_full", (6, 7))
                    if prev is not None and t == 5:
                        logits(prev)
                    if prev is not None and t == 7:
                        ranks(prev)
                    if t >= 1:
                        pe.wait_ge(sm["k_relu"], b * 2 * T + 2 * t)
                        for k in range(2):
                            ins = pe.matmul(bank[2 + k][:, :], h_sb[:, t - 1, :],
                                            kf[:, (t - 1) % 2, k * 512:k * 512 + 512], start=t == 1, stop=t == T)
                        ins.then_inc(sm["g_done"], 1)

            def logits(b):
                pe.wait_ge(sm["h2t_copied"], b * G + G)
                for t in range(T):
                    ins = pe.matmul(bank[5][:, t * E:(t + 1) * E], h2t[:, t * P:(t + 1) * P], wr_t[:, :],
                                    start=True, stop=True)
                ins.then_inc(sm["logit_full"], 1)

            def ranks(b):
                pe.wait_ge(sm["picks_ready"], b + 1)
                rank = bank[5][:, 64:128]
                pe.matmul(rank, lower_bf[:, :], picks_bf[:, T - 1:, :], start=True, stop=False)
                for back in range(1, T):
                    pe.matmul(rank, ones_bf[:, :], picks_bf[:, T - 1 - back:2 * T - 1 - back, :], start=False,
                              stop=back == T - 1)
                for t in range(T):
                    ins = pe.matmul(bank[6][:, 0:E], ones_bf[:, :], picks_bf[:, T - 1 + t, :], start=t == 0,
                                    stop=t == T - 1)
                ins.then_inc(sm["rank_full"], 1)

            def q_features(b, g):
                for j in range(NJ):
                    i = NJ * g + j
                    if i >= 3:
                        pe.wait_ge(sm["q_ready"], b * G * NJ + i - 2)
                    f, tok = slice(j * P, (j + 1) * P), slice(g * 512, g * 512 + 512)
                    product(bank[Z[i % 3]][:, :], wqk_hi[:, 0, f], wqk_lo[:, 0, f], ht_hi[:, tok], ht_lo[:, tok]
                            ).then_inc(sm["q_full"], 1)

            def norms(b, g):
                if g:
                    pe.wait_ge(sm["norm_copied"], b * G + g)
                for j in range(NJ):
                    pe.wait_ge(sm["q_ready"], b * G * NJ + NJ * g + j + 1)
                    ins = pe.matmul(bank[5][0:H, :], ks_bd[:, j, :], q_act[:, g, j, :], start=j == 0,
                                    stop=j == NJ - 1)
                ins.then_inc(sm["norm_full"], 1)

            def norms_t(b, g):
                pe.wait_ge(sm["norm_copied"], b * G + g + 1)
                for i in range(4):
                    ins = pe.matmul(bank[6 + g][:, H * i:H * i + H], norm_sb[:, i * P:(i + 1) * P],
                                    ident[0:H, 0:H], start=True, stop=True)
                ins.then_inc(sm["normt_full"], 1)

            def recips_t(b, g):
                pe.wait_ge(sm["r_ready"], b * G + g + 1)
                pe.transpose(bank[6 + g][0:32, 0:P], recip[:, 0, 0:32], ident[:, :])
                for i in range(4):
                    ins = pe.transpose(bank[6 + g][0:64, i * P:(i + 1) * P], recip[:, i, :], ident[:, :])
                ins.then_inc(sm["rt_full"], 1)

            def queries(b, prev):
                q_features(b, 0)
                if prev is not None:
                    pe.wait_ge(sm["route_ready"], prev + 1)
                pe.wait_ge(sm["k_added"], b * (T - 1) + T - 1)
                for j in range(NJ):
                    ins = pe.matmul(bank[5][:, j:j + 1], k_sum[:, j * P:(j + 1) * P], ones_col[:, :],
                                    start=True, stop=True)
                ins.then_inc(sm["ksum_full"], 1)
                pe.wait_ge(sm["gt_copied"], b * 2 + 2)
                for k in range(4):
                    for i in range(2):
                        j = 2 * k + i
                        ins = pe.matmul(bank[MB[k]][:, i * 256:(i + 1) * 256], gt_sb[:, j * P:(j + 1) * P],
                                        vo[:, 2 * j:2 * j + 2, :], start=True, stop=True)
                    ins.then_inc(sm["m_full"], 1)
                q_features(b, 1)
                pe.wait_ge(sm["ks_ready"], b + 1)
                pe.wait_ge(sm["m_copied"], b * 4 + 4)
                norms(b, 0)
                norms_t(b, 0)
                norms(b, 1)
                recips_t(b, 0)
                norms_t(b, 1)

            def attend(b, g, between=None):
                pe.wait_ge(sm["r_lo"], b * G + g + 1)
                for j in range(NJ + 1):
                    if j < NJ:
                        i = NJ * g + j
                        if i >= 2:
                            pe.wait_ge(sm["qn_ready"], b * G * NJ + i - 1)
                        pe.matmul(bank[2 + i % 2][:, :], sel[:, j, :], r_parts[:, g, :], start=True, stop=True
                                  ).then_inc(sm["rb_full"], 1)
                    if j >= 1:
                        i = NJ * g + j - 1
                        pe.wait_ge(sm["qn_ready"], b * G * NJ + i + 1)
                        pe.matmul(bank[4 + g][:, :], m_sb[:, j - 1, :], qn[:, i % 2, :], start=j == 1,
                                  stop=j == NJ).then_inc(sm["out_done"], 1)

            def experts(b):
                def tokens_t(q):
                    pe.wait_ge(hs_in[q], b * 16 + 16)
                    if q >= 2:
                        pe.wait_ge(sm["ft_lo"], b * NQ + q - 1)
                    for i, s in enumerate(quad(q)):
                        ins = pe.transpose(bank[FT[q % 2]][:, i * P:(i + 1) * P], hs[:, s, :], ident[:, :])
                    ins.then_inc(sm["ft_full"], 1)

                tokens_t(0)
                pe.wait_ge(sm["owner_ready"], b + 1)
                expert = {}
                for i in range(S + 2):
                    if i < S:
                        if i % 4 == 0 and i // 4 + 1 < NQ:
                            tokens_t(i // 4 + 1)
                        expert[i] = pe.value_load(owner_i[0:1, i:i + 1], min_val=0, max_val=E - 1)
                        pe.wait_ge(sm["ft_lo"], b * NQ + i // 4 + 1)
                        if i >= 2:
                            pe.wait_ge(sm["hid_ready"], b * S + i - 1)
                        tok = slice((i % 4) * P, (i % 4 + 1) * P)
                        cols = bass.ds(expert[i] * (2 * F), 2 * F)
                        product(bank[i % 2][:, :], hst_hi[:, (i // 4) % 2, tok], hst_lo[:, (i // 4) % 2, tok],
                                wgu_hi[:, cols], wgu_lo[:, cols]).then_inc(sm["gu_full"], 1)
                    if 1 <= i <= S:
                        k = i - 1
                        pe.wait_ge(sm["hid_ready"], b * S + k + 1)
                        if k >= 2:
                            pe.wait_ge(sm["hidt_copied"], b * S + k - 1)
                        for f in range(2):
                            ins = pe.transpose(bank[HT[k % 2]][:, f * P:(f + 1) * P],
                                               hid[:, k % 2, f * P:(f + 1) * P], ident[:, :])
                        ins.then_inc(sm["hidt_full"], 1)
                    if i >= 2:
                        k = i - 2
                        pe.wait_ge(sm["hidt_copied"], b * S + k + 1)
                        if k >= 2:
                            pe.wait_ge(sm["y_copied"], b * S + k - 1)
                        for f in range(2):
                            ins = pe.matmul(bank[YB[k % 2]][:, 0:P], hid_t[:, k % 2, f * P:(f + 1) * P],
                                            wd[:, bass.ds(expert[k] * (2 * P) + f * P, P)], start=f == 0, stop=f == 1)
                        ins.then_inc(sm["y_full"], 1)

            def batch(b, prev, last=False):
                pe.wait_ge(sm["ht_dve"], b * G + G)
                keys(b, prev)
                queries(b, prev)
                if prev is not None:
                    experts(prev)
                if not last:
                    transposes(b + 1, "h_ready", h_sb, "ht_full", (0, 1))
                attend(b, 0)
                recips_t(b, 1)
                attend(b, 1)
                for g in range(G):
                    pe.wait_ge(sm["at_copied"], b * G + g + 1)
                    for i in range(4):
                        ins = pe.transpose(bank[6 + g][:, i * P:(i + 1) * P], at_sb[:, g, i * P:(i + 1) * P],
                                           ident[:, :])
                    ins.then_inc(sm["att_full"], 1)

            transposes(0, "h_ready", h_sb, "ht_full", (0, 1))
            batch(0, None)
            with pe.Fori(1, B - 1) as b:
                batch(b, b - 1)
            batch(B - 1, B - 2, last=True)
            transposes(B - 1, "h2_ready", h2, "h2t_full", (6, 7))
            logits(B - 1)
            ranks(B - 1)
            experts(B - 1)


_INS = ['L0_attn_x', 'L0_attn_W_qkv', 'L0_attn_W_f', 'L0_attn_b_f', 'L0_attn_W_out', 'L0_attn_b_out',
        'L0_ffn_w_router', 'L0_ffn_w_gate', 'L0_ffn_w_up', 'L0_ffn_w_down', 'L0_ffn_ln_gamma', 'L0_ffn_ln_beta',
        'L0_c', 'L0_wmod']


def kernel(**inputs):
    import numpy as np
    import concourse.bacc as bacc
    from concourse import mybir as mb
    from concourse.bass_utils import run_bass_kernel_spmd

    nc = bacc.Bacc("TRN2", target_bir_lowering=False, num_devices=1)
    arrays, args = {}, []
    for name in _INS:
        a = np.ascontiguousarray(inputs[name])
        arrays[f"in_{name}"] = a
        args.append(nc.dram_tensor(f"in_{name}", a.shape, mb.dt.from_np(a.dtype), kind="ExternalInput").ap())
    shape = inputs['L0_attn_x'].shape
    args.append(nc.dram_tensor("out_x", shape, mb.dt.float32, kind="ExternalOutput").ap())
    build_block(nc, *args)
    r = run_bass_kernel_spmd(nc, [arrays], core_ids=[0])
    return r.results[0]["out_x"]
```

```python
from contextlib import ExitStack

import concourse.bass as bass
from concourse import mybir

ALU = mybir.AluOpType
ACT = mybir.ActivationFunctionType
F32 = mybir.dt.float32
F32R = mybir.dt.float32r
BF16 = mybir.dt.bfloat16
U32 = mybir.dt.uint32
AX_X = mybir.AxisListType.X
P = 128


def build_block(nc, x, wqkv, wf, bf, wout, bout, wrouter, wgate, wup, wdown, gamma, beta, cond, wmod, out):
    B, N, C = x.shape
    D = wf.shape[0]
    INNER = wout.shape[0]
    H = INNER // D
    E, F, _ = wgate.shape
    T = N // P
    G = T // 4
    NJ = INNER // P
    S = (2 * N + E * (P - 1)) // P
    NQ = (S + 3) // 4
    W = -(-S // 8)
    EPS = 1e-5
    BIG = 3.0e38
    assert C == P and D == 64 and H == 2 * NJ and F == 2 * P and T == 8 and E == 8 and G == 2

    ctx = ExitStack()
    with ctx:
        def sb(name, shape, dt=F32):
            return ctx.enter_context(nc.sbuf_tensor(name, shape, dt))

        def sem(name):
            return ctx.enter_context(nc.semaphore(name))

        ident = sb("ident", [P, P])
        lower_bf = sb("lower_bf", [P, P], BF16)
        ones_bf = sb("ones_bf", [P, P], BF16)
        ones_col = sb("ones_col", [P, 1])
        sel = sb("sel", [P, NJ, P], F32R)
        head_mask = sb("head_mask", [P, NJ, H])
        iota_e = sb("iota_e", [P, T, E])
        step128 = sb("step128", [P, E, T])
        before = sb("before", [P, E, E])
        iota_s = sb("iota_s", [P, S, E])
        neg_half = sb("neg_half", [P, T])
        nothing = sb("nothing", [P, 1])

        wqk_hi = sb("wqk_hi", [P, 2, INNER], F32R)
        wqk_lo = sb("wqk_lo", [P, 2, INNER], F32R)
        vo = sb("vo", [P, H, P])
        wgu_hi = sb("wgu_hi", [P, E * 2 * F], F32R)
        wgu_lo = sb("wgu_lo", [P, E * 2 * F], F32R)
        wd = sb("wd", [P, E * 2 * P])
        wr_t = sb("wr_t", [P, E])
        bf_col = sb("bf_col", [P, 1])
        bf_row = sb("bf_row", [P, D])
        gamma_row = sb("gamma_row", [P, P])
        beta_row = sb("beta_row", [P, P])
        mod = sb("mod", [P, B * 6 * P])
        bout_col = sb("bout_col", [P, 1])
        ga_col = sb("ga_col", [P, B, 2])

        q_act = sb("q_act", [P, G, NJ, 4 * P])
        flat = q_act[:, :, :, :].rearrange("p g j n -> p (g j n)")
        wqkv_nat = flat[:, 0:3 * INNER]
        wg_nat = flat[:, 3072:5120].rearrange("p (k c) -> p k c", c=P)
        wu_nat = flat[:, 5120:7168].rearrange("p (k c) -> p k c", c=P)
        hs = sb("hs", [P, S, P])
        y_sb = hs
        arena_k = sb("arena_k", [P, 3 * INNER])
        arena_x = sb("arena_x", [P, 2 * INNER])
        arena_a = sb("arena_a", [P, 2 * INNER])
        arena_t = sb("arena_t", [P, 2 * INNER])
        wd_nat = arena_a[:, :].rearrange("p (e f) -> p e f", e=E)
        wt = arena_k[:, :].rearrange("p (k c) -> p k c", c=P)
        wo_bd = arena_x[:, :].rearrange("p (j c) -> p j c", c=2 * P)
        sel_f = arena_t[:, 0:INNER].rearrange("p (j c) -> p j c", c=P)
        wmod_sb = arena_t[:, INNER:INNER + 6 * P]
        c_t = sb("c_t", [P, B])

        x_sb = arena_x[:, 0:INNER].rearrange("p (t c) -> p t c", c=P)
        h_sb = arena_x[:, INNER:2 * INNER].rearrange("p (t c) -> p t c", c=P)
        ht_hi = sb("ht_hi", [P, T * P], F32R)
        ht_lo = sb("ht_lo", [P, T * P], F32R)
        kf = arena_k[:, 0:2 * INNER].rearrange("p (a n) -> p a n", a=2)
        k_sum = arena_k[:, 2 * INNER:3 * INNER]
        gt_sb = sb("gt_sb", [P, INNER])
        m_sb = sb("m_sb", [P, NJ, P])
        ks_parts = sb("ks_parts", [P, NJ, 3 * H], F32R)
        fold = sb("fold", [2 * H, H])
        norm_sb = sb("norm_sb", [2 * H, 4 * P])
        recip_in = sb("recip_in", [P, 4, H])
        recip = sb("recip", [P, 4, 2 * 32])
        r_parts = sb("r_parts", [P, G, 4 * P], F32R)
        c_b = gt_sb[:, 0:B * P].rearrange("p (b c) -> p b c", c=P)
        qn = arena_a[:, 0:INNER].rearrange("p (a n) -> p a n", a=2)
        at_sb = arena_a[:, INNER:2 * INNER].rearrange("p (a n) -> p a n", a=2)
        ga_now = sb("ga_now", [P, 2])
        h2 = arena_a[:, INNER:2 * INNER].rearrange("p (t c) -> p t c", c=P)
        res = arena_t[:, 0:INNER].rearrange("p (t c) -> p t c", c=P)
        x2 = arena_t[:, INNER:2 * INNER].rearrange("p (t c) -> p t c", c=P)
        h2t = flat[:, 0:T * P]
        norm_of = {}
        for k in (1, 2, 3):
            norm_of[k] = (sb(f"stats{k}", [P, T, 6]), sb(f"mv{k}", [P, T, 2]), sb(f"var_e{k}", [P, T]),
                          sb(f"rstd{k}", [P, T]), sb(f"shift{k}", [P, T]))
        logit = sb("logit", [P, T, E])
        code = sb("code", [P, T, E])
        eq = sb("eq", [P, T, E])
        pick1 = sb("pick1", [P, T, E])
        pick2 = sb("pick2", [P, T, E])
        picks_bf = sb("picks_bf", [P, 2 * T - 1, E], BF16)
        top1 = sb("top1", [P, T])
        top2 = sb("top2", [P, T])
        first = sb("first", [P, T])
        gap = sb("gap", [P, T])
        th = sb("th", [P, T])
        w1 = sb("w1", [P, 2, T])
        w2 = sb("w2", [P, 2, T])
        over = sb("over", [P, E, T])
        n_tiles = sb("n_tiles", [P, E])
        prior = sb("prior", [P, E, E])
        tile0 = sb("tile0", [P, E])
        tile1 = sb("tile1", [P, E])
        passed = flat[:, 7168:7168 + S * E].rearrange("p (s e) -> p s e", e=E)
        owner = sb("owner", [P, W * 8])
        coded = sb("coded", [P, W, 8])
        owners = sb("owners", [P, W])
        owners_i = sb("owners_i", [P, 2, W], U32)
        octal = sb("octal", [P, W, 8])
        slot = sb("slot", [P, T, E])
        slot_p = sb("slot_p", [P, T, E])
        slots = sb("slots", [P, 2 * T])
        slots_i = sb("slots_i", [P, 2, 2 * T], U32)
        hst_hi = sb("hst_hi", [P, 2, 4 * P], F32R)
        hst_lo = sb("hst_lo", [P, 2, 4 * P], F32R)

        def q_part(i, lo):
            at = (i + 1) % 3
            return (hst_lo if lo else hst_hi)[:, at, :] if at < 2 else r_parts[:, lo, :]

        gate = sb("gate", [P, 2, F])
        hid = sb("hid", [P, 2, F])
        ks_bd = gate[:, 0, 0:NJ * H].rearrange("p (j h) -> p j h", h=H)
        hid_t = sb("hid_t", [P, 2, F])
        wf_bd = hid[:, 0, 0:P]
        wr_nat = hid[0:E, 1, 0:P]
        c_nat = hid[0:B, 1, P:2 * P]
        sign_b = gate[:, :, :].rearrange("p a (b c) -> p (a b) c", c=P)
        y1 = kf[:, 0, :].rearrange("p (t c) -> p t c", c=P)
        y2 = kf[:, 1, :].rearrange("p (t c) -> p t c", c=P)
        y = gt_sb[:, :].rearrange("p (t c) -> p t c", c=P)
        x_first = flat[:, 7168:8192].rearrange("p (t c) -> p t c", c=P)
        x2_end = x_sb
        hs_end = flat[:, 4096:4096 + S * P].rearrange("p (s c) -> p s c", c=P)

        bank = [ctx.enter_context(nc.psum_tensor(f"bank{i}", [P, 512], F32)) for i in range(8)]

        rows_in = nc.dram_tensor("rows_in", [S * P, P], F32, kind="Internal").ap()
        rows_out = nc.dram_tensor("rows_out", [S * P, P], F32, kind="Internal").ap()

        ident_ready = sem("ident_ready")
        const_ready = sem("const_ready")
        zeroed, wo_zeroed, hs_zeroed = sem("zeroed"), sem("wo_zeroed"), sem("hs_zeroed")
        in_qkv, in_heads, in_gu, in_down, in_cond, in_rows = (
            sem(n) for n in ("in_qkv", "in_heads", "in_gu", "in_down", "in_cond", "in_rows"))
        su_full, su_act, su_dve = sem("su_full"), sem("su_act"), sem("su_dve")
        sel_ready, c_wide = sem("sel_ready"), sem("c_wide")
        held = sem("held")
        pool_chain = sem("pool_chain")
        dve_chain = sem("dve_chain")
        names = """x_in x_used var1 rstd1 var2 rstd2 var3 rstd3 h_scaled h_ready w_ready ht_full ht_act ht_dve
            k_full k_biased k_relu g_done k_added q_full q_ready gt_copied ksum_full ks_ready m_full m_copied q_lo
            q_normed norm_copied normt_full r_ready rt_full r_hi r_lo rb_full qn_ready out_done at_copied att_full
            x2_ready shift2 shift3 normed2 normed3 y_modulated h2_ready h2t_full h2t_copied logit_full gap_ready
            tanh_done picks_ready rank_full owner_ready route_ready scattered ft_full ft_hi ft_lo gu_full silu_done
            hid_ready hidt_full hidt_copied y_full y_copied y_stored y1_weighed y_taken res_ready stored""".split()
        sm = {n: sem(n) for n in names}
        hs_in = [sem(f"hs_in{q}") for q in range(NQ)]
        gathered = [sem(f"gathered{g}") for g in range(G)]

        Z = (0, 1, 4)
        NB = (5, 3)
        HB = (6, 7)
        MB = (6, 7, 2, 3)
        FT, HT, YB = 2, 3, (4, 5)
        SETUP_JOBS = 2 + 6 + 2 * B + 4 + 4 + E + G + 4

        def quad(q):
            return range(4 * q, min(4 * q + 4, S))

        block = ctx.enter_context(nc.Block())

        @block.sync
        def _(sp):
            sp.dma_start(wqkv_nat, wqkv).then_inc(in_qkv, 16)
            x_flat, out_flat = x.rearrange("b n c -> (b n c)"), out.rearrange("b n c -> (b n c)")
            sp.dma_start(x_first[:, :, :], x_flat[0:N * C].rearrange("(t p c) -> p t c", p=P, c=C)
                         ).then_inc(sm["x_in"], 16)
            sp.wait_ge(zeroed, 1)
            sp.wait_ge(wo_zeroed, 1)
            for s in range(2):
                lo, hi = s * D, (s + 1) * D
                sp.dma_start(wf_bd[lo:hi, lo:hi], wf).then_inc(in_heads, 16)
                sp.dma_start(wo_bd[lo:hi, :, s * P:(s + 1) * P],
                             wout.rearrange("(j s e) d -> s e j d", s=2, e=D)[s]).then_inc(in_heads, 16)
                sp.dma_start(bf_col[lo:hi, :], bf.rearrange("(e a) -> e a", a=1)).then_inc(in_rows, 16)
            sp.dma_start(wd_nat, wdown.rearrange("e d f -> d e f")).then_inc(in_down, 16)
            for row, src in ((bf_row, bf), (gamma_row, gamma), (beta_row, beta)):
                sp.dma_start(row[:, :], src.partition_broadcast(P)).then_inc(in_rows, 16)
            sp.dma_start(bout_col[:, :], bout.rearrange("(e a) -> e a", a=1)).then_inc(in_rows, 16)
            sp.wait_ge(hs_zeroed, 1)
            sp.dma_start(rows_in.rearrange("(s p) c -> p s c", p=P), hs[:, :, :]).then_inc(sm["stored"], 16)

            def load_x(b):
                at = bass.ds(b * (N * C), N * C)
                sp.dma_start(x_sb[:, :, :], x_flat[at].rearrange("(t p c) -> p t c", p=P, c=C)
                             ).then_inc(sm["x_in"], 16)

            def load_rows(b, dst):
                sp.wait_ge(sm["scattered"], b * (32 * T) + 32 * T)
                for q in range(NQ):
                    n = len(quad(q))
                    sp.dma_start(dst[:, 4 * q:4 * q + n, :],
                                 rows_in[4 * q * P:(4 * q + n) * P, :].rearrange("(s p) c -> p s c", p=P)
                                 ).then_inc(hs_in[q], 16)

            def store_rows(b):
                for q in range(NQ):
                    n = len(quad(q))
                    sp.wait_ge(sm["y_copied"], b * S + 4 * q + n)
                    sp.dma_start(rows_out[4 * q * P:(4 * q + n) * P, :].rearrange("(s p) c -> p s c", p=P),
                                 y_sb[:, 4 * q:4 * q + n, :]).then_inc(sm["y_stored"], 16)

            def store(b):
                at = bass.ds(b * (N * C), N * C)
                sp.wait_ge(sm["res_ready"], b + 1)
                sp.dma_start(out_flat[at].rearrange("(t p c) -> p t c", p=P, c=C), res[:, :, :]
                             ).then_inc(sm["stored"], 16)

            def load_again(b):
                sp.wait_ge(sm["x_used"], b + 2)
                load_x(b)

            def step(b, prev):
                sp.wait_ge(sm["x2_ready"], prev * G + G)
                load_x(b + 1)
                load_rows(prev, hs)
                store_rows(prev)
                load_again(b)
                store(prev)

            sp.wait_ge(su_act, SETUP_JOBS)
            load_x(1)
            load_again(0)
            with sp.Fori(1, B - 1) as b:
                step(b, b - 1)
            sp.wait_ge(sm["x2_ready"], (B - 2) * G + G)
            load_x(B - 1)
            load_rows(B - 2, hs)
            store_rows(B - 2)
            load_rows(B - 1, hs_end)
            for g in range(G):
                sp.wait_ge(gathered[g], (B - 1) * 16 * T)
            store(B - 2)
            store_rows(B - 1)
            store(B - 1)
            sp.wait_ge(sm["stored"], 16 * B + 16)

        @block.gpsimd
        def _(pool):
            n = [0]

            def link(ins):
                n[0] += 1
                ins.then_inc(pool_chain, 1)
                pool.wait_ge(pool_chain, n[0])

            pool.memset(neg_half[:, :], -0.5)
            pool.memset(nothing[:, :], 0.0)
            pool.memset(wf_bd[:, :], 0.0).then_inc(zeroed, 1)
            link(pool.memset(ident[:, :], 0.0))
            pool.affine_select(out=ident[:, :], in_=ident[:, :], compare_op=ALU.not_equal, fill=1.0, base=0,
                               pattern=[[-1, P]], channel_multiplier=1).then_inc(ident_ready, 1)
            pool.memset(lower_bf[:, :], 1.0)
            pool.memset(ones_bf[:, :], 1.0)
            pool.memset(sel_f[:, :, :], 0.0)
            pool.memset(head_mask[:, :, :], 0.0)
            pool.memset(before[:, :, :], 1.0)
            link(pool.memset(iota_e[:, :, :], 0.0))

            def select(ap, compare, fill, base, pattern, per_row):
                link(pool.affine_select(out=ap, in_=ap, compare_op=compare, fill=fill, base=base,
                                        pattern=pattern, channel_multiplier=per_row))
            select(lower_bf[:, :], ALU.is_gt, 0.0, 0, [[1, P]], -1)
            sel_v = sel_f[:, :, :].rearrange("p j (s e) -> p j s e", s=2)
            for base in (0, -32):
                select(sel_v, ALU.not_equal, 1.0, base, [[-2, NJ], [-1, 2], [0, D]], 1)
            for s in range(2):
                select(head_mask[s * D:(s + 1) * D, :, :], ALU.not_equal, 1.0, -s, [[-2, NJ], [1, H]], 0)
            select(before[:, :, :], ALU.is_gt, 0.0, 0, [[1, E], [-1, E]], 0)
            pool.iota(iota_e[:, :, :], [[0, T], [1, E]], base=0, channel_multiplier=0,
                      allow_small_or_imprecise_dtypes=True)
            pool.iota(step128[:, :, :], [[0, E], [P, T]], base=0, channel_multiplier=0,
                      allow_small_or_imprecise_dtypes=True)
            link(pool.iota(iota_s[:, :, :], [[1, S], [0, E]], base=0, channel_multiplier=0,
                           allow_small_or_imprecise_dtypes=True))
            pool.memset(ones_col[:, :], 1.0).then_inc(const_ready, 1)

            def rsqrt(k, b):
                _, _, var_e, rstd, _ = norm_of[k]
                pool.wait_ge(sm[f"var{k}"], b + 1)
                pool.tensor_tensor(rstd[:, :], var_e[:, :], neg_half[:, :], ALU.pow).then_inc(sm[f"rstd{k}"], 1)

            def hold(name, value):
                pool.wait_ge(sm[name], value)
                pool.tensor_tensor(nothing[:, :], nothing[:, :], nothing[:, :], ALU.add).then_inc(held, 1)

            def sum_keys(b, routed=None, combined=None):
                if routed is not None:
                    rsqrt(2, routed)
                for t in range(1, T):
                    if t == 3 and combined is not None:
                        rsqrt(3, combined)
                    if t == 7 and combined is not None:
                        pool.wait_ge(sm["y_modulated"], combined + 1)
                        pool.tensor_tensor(res[:, :, :], y[:, :, :], res[:, :, :], ALU.add
                                           ).then_inc(sm["res_ready"], 1)
                    pool.wait_ge(sm["k_relu"], b * 2 * T + 2 * t + 2)
                    if t >= 2:
                        pool.wait_ge(sm["k_added"], b * (T - 1) + t - 1)
                    pool.tensor_tensor(k_sum[:, :], kf[:, 0, :] if t == 1 else k_sum[:, :], kf[:, t % 2, :],
                                       ALU.add).then_inc(sm["k_added"], 1)

            def scatter(b, end=0):
                if not (isinstance(b, int) and b == 0):
                    pool.wait_ge(held, 2 * B - 3 if end else b * 2)
                hold("route_ready", b + 1)
                for t in range(T):
                    for k in range(2):
                        at = slots_i[:, end, k * T + t:k * T + t + 1]
                        pool.indirect_dma_start(out=rows_in, out_offset=bass.IndirectOffsetOnAxis(at, 0),
                                                in_=h2[:, t, :], in_offset=None).then_inc(sm["scattered"], 16)

            def gather(b, end=0):
                pool.wait_ge(held, 2 * B - 1 if end else (2 * B - 2 if isinstance(b, int) else b * 2 + 1))
                hold("y_stored", b * (16 * NQ) + 16 * NQ)
                for t in range(T):
                    for k, y_k in enumerate((y1, y2)):
                        at = slots_i[:, end, k * T + t:k * T + t + 1]
                        pool.indirect_dma_start(out=y_k[:, t, :], out_offset=None, in_=rows_out,
                                                in_offset=bass.IndirectOffsetOnAxis(at, 0)
                                                ).then_inc(gathered[t // 4], 16)

            rsqrt(1, 0)
            pool.wait_ge(sm["stored"], 16)
            sum_keys(0)
            rsqrt(1, 1)
            sum_keys(1, 0)
            scatter(0)
            with pool.Fori(1, B - 1) as b:
                rsqrt(1, b + 1)
                gather(b - 1)
                sum_keys(b + 1, b, b - 1)
                scatter(b)
            rsqrt(2, B - 1)
            for q in range(NQ):
                pool.wait_ge(hs_in[q], (B - 1) * 16)
            scatter(B - 1, 1)
            gather(B - 2)
            rsqrt(3, B - 2)
            pool.wait_ge(sm["y_taken"], (B - 1) * G)
            gather(B - 1, 1)
            rsqrt(3, B - 1)

        @block.scalar
        def _(act):
            act.dma_start(c_nat[:, :], cond).then_inc(in_cond, 16)
            act.dma_start(wmod_sb[:, :], wmod).then_inc(in_cond, 16)
            act.dma_start(wr_nat[:, :], wrouter).then_inc(in_cond, 16)
            act.dma_start(wg_nat, wgate.rearrange("e (k p) c -> p (e k) c", p=P)).then_inc(in_gu, 16)
            act.dma_start(wu_nat, wup.rearrange("e (k p) c -> p (e k) c", p=P)).then_inc(in_gu, 16)
            job = [0]

            def evac(dst):
                act.wait_ge(su_full, job[0] + 1)
                src = bank[job[0] % 8][:, 0:512]
                act.activation(dst, src, ACT.Copy).then_inc(su_act, 1)
                job[0] += 1

            act.wait_ge(su_full, 1)
            act.activation(wr_t[:, :], bank[0][:, 0:E], ACT.Copy)
            act.activation(c_t[:, :], bank[0][:, 16:16 + B], ACT.Silu).then_inc(su_act, 1)
            act.wait_ge(su_act, 1)
            for b in range(B):
                act.activation(c_b[:, b, :], c_t[:, b:b + 1].to_broadcast([P, P]), ACT.Copy).then_inc(c_wide, 1)
            job[0] = 1
            act.wait_ge(su_full, 2)
            act.activation(ga_col[:, :, 0], bank[1][:, 0:B], ACT.Copy).then_inc(su_act, 1)
            job[0] = 2
            for k in range(6):
                evac(wt[:, 4 * k:4 * k + 4, :])
            for k in range(2 * B):
                half = mod[:, (k // 2) * 768 + (k % 2) * 384:(k // 2) * 768 + (k % 2) * 384 + 384]
                act.wait_ge(su_full, job[0] + 1)
                act.activation(half, bank[job[0] % 8][:, 0:384], ACT.Copy).then_inc(su_act, 1)
                job[0] += 1
            for k in range(4):
                evac(wqk_hi[:, k // 2, (k % 2) * 512:(k % 2) * 512 + 512])
            for k in range(4):
                evac(vo[:, 4 * k:4 * k + 4, :])
            for e in range(E):
                if e == E // 2:
                    for g in range(G):
                        evac(ht_hi[:, g * 512:g * 512 + 512])
                evac(wgu_hi[:, e * 512:e * 512 + 512])
            for k in range(4):
                evac(wd[:, k * 512:k * 512 + 512])

            def transposed(b):
                for g in range(G):
                    act.wait_ge(sm["ht_full"], b * G - G + g + 1)
                    act.activation(ht_hi[:, g * 512:g * 512 + 512], bank[HB[g]][:, :], ACT.Copy
                                   ).then_inc(sm["ht_act"], 1)

            def normalise(k, b, dst, src):
                _, _, _, rstd, shift_k = norm_of[k]
                act.wait_ge(sm[f"shift{k}"], b + 1)
                for t in range(T):
                    ins = act.activation(dst[:, t, :], src[:, t, :], ACT.Identity, scale=rstd[:, t:t + 1],
                                         bias=shift_k[:, t:t + 1])
                ins.then_inc(sm[f"normed{k}"], 1)

            def keys(b, routed=None, combined=None):
                for i in range(2 * T):
                    act.wait_ge(sm["k_biased"], b * 2 * T + i + 1)
                    half = kf[:, (i // 2) % 2, (i % 2) * 512:(i % 2) * 512 + 512]
                    act.activation(half, half, ACT.Relu).then_inc(sm["k_relu"], 1)
                    if routed is not None and i == 2 * 1 + 1:
                        normalise(2, routed, h2, x2)
                    if routed is not None and i == 2 * 4 + 1:
                        tokens_copied(routed)
                    if combined is not None and i == 2 * 4 + 1:
                        normalise(3, combined, y, y)
                    if routed is not None and i == 2 * 6 + 1:
                        gap_tanh(routed)

            def tokens_copied(b):
                for g in range(G):
                    act.wait_ge(sm["h2t_full"], b * G + g + 1)
                    act.activation(h2t[:, g * 512:g * 512 + 512], bank[6 + g][:, :], ACT.Copy
                                   ).then_inc(sm["h2t_copied"], 1)

            def gap_tanh(b):
                act.wait_ge(sm["gap_ready"], b + 1)
                act.activation(th[:, :], gap[:, :], ACT.Tanh, scale=0.5).then_inc(sm["tanh_done"], 1)

            def q_relu(b, i):
                z = bank[Z[i % 3]][:, :]
                act.wait_ge(sm["q_full"], b * G * NJ + i + 1)
                act.activation(q_act[:, i // NJ, i % NJ, :], z, ACT.Relu, bias=bf_col[:, 0:1])
                if i >= 3:
                    act.wait_ge(sm["q_normed"], b * G * NJ + i - 2)
                act.activation(q_part(i, 0), z, ACT.Relu, bias=bf_col[:, 0:1]).then_inc(sm["q_ready"], 1)

            def norms(b, g):
                act.wait_ge(sm["q_normed"], b * G * NJ + NJ * (g + 1))
                if g:
                    act.wait_ge(sm["normt_full"], b * G + g)
                act.activation(norm_sb[:, :], bank[NB[g]][0:2 * H, :], ACT.Copy).then_inc(sm["norm_copied"], 1)

            def recips(b, g):
                act.wait_ge(sm["rt_full"], b * G + g + 1)
                act.activation(r_parts[0:64, g, :], bank[6 + g][0:64, :], ACT.Copy).then_inc(sm["r_hi"], 1)

            def rows_copied(b, q):
                w = len(quad(q)) * P
                act.wait_ge(sm["ft_full"], b * NQ + q + 1)
                if q >= 2:
                    act.wait_ge(sm["gu_full"], b * S + 4 * q - 4)
                act.activation(hst_hi[:, q % 2, 0:w], bank[FT][:, 0:w], ACT.Copy).then_inc(sm["ft_hi"], 1)

            def queries(b, combined=None, routed=None):
                act.wait_ge(sm["g_done"], b * T + T)
                if combined is not None:
                    act.wait_ge(sm["res_ready"], combined + 1)
                for k in range(2):
                    act.activation(gt_sb[:, k * 512:k * 512 + 512], bank[2 + k][:, :], ACT.Copy
                                   ).then_inc(sm["gt_copied"], 1)
                for i in range(G * NJ):
                    q_relu(b, i)
                    if i == 10:
                        norms(b, 0)
                if routed is not None:
                    act.wait_ge(sm["q_normed"], b * G * NJ + G * NJ - 1)
                    rows_copied(routed, 0)

            def experts(b, during=None, routed=None, combined=None):
                if routed is None and during is None:
                    rows_copied(b, 0)
                if during is not None:
                    norms(during, 1)
                for i in range(S + 1):
                    if i < S:
                        if i % 4 == 0 and i // 4 + 1 < NQ:
                            rows_copied(b, i // 4 + 1)
                        act.wait_ge(sm["gu_full"], b * S + i + 1)
                        if i >= 2:
                            act.wait_ge(sm["hid_ready"], b * S + i - 1)
                        act.activation(gate[:, i % 2, :], bank[i % 2][:, 0:F], ACT.Silu).then_inc(sm["silu_done"], 1)
                    if i >= 1:
                        act.wait_ge(sm["hidt_full"], b * S + i)
                        if i >= 3:
                            act.wait_ge(sm["y_full"], b * S + i - 2)
                        act.activation(hid_t[:, (i - 1) % 2, :], bank[HT][:, 0:F], ACT.Copy
                                       ).then_inc(sm["hidt_copied"], 1)
                    if during is not None and i in (2, 4):
                        recips(during, i // 4)
                    if routed is not None and i == 5:
                        tokens_copied(routed)
                    if routed is not None and i == 9:
                        gap_tanh(routed)
                    if combined is not None and i in (9, 10):
                        weigh(combined, i - 9)

            def weigh(b, g, end=0):
                act.wait_ge(sm["w_ready"], b + 1)
                act.wait_ge(gathered[g], b * (16 * T) + 16 * T)
                for t in range(4 * g, 4 * g + 4):
                    ins = act.activation(y[:, t, :], y1[:, t, :], ACT.Copy, scale=w1[:, end, t:t + 1])
                ins.then_inc(sm["y1_weighed"], 1)

            def attended(b, scattered=None, gathered_b=None, nxt=None):
                if nxt is not None:
                    transposed(nxt)
                if scattered is not None:
                    act.wait_ge(sm["scattered"], scattered * (32 * T) + 32 * T)
                for g in range(G):
                    act.wait_ge(sm["out_done"], b * G * NJ + NJ * (g + 1))
                    act.activation(at_sb[:, g, :], bank[4 + g][:, :], ACT.Identity, scale=ga_now[:, 0:1],
                                   bias=ga_now[:, 1:2]).then_inc(sm["at_copied"], 1)
                    if gathered_b is not None:
                        weigh(gathered_b, g)

            keys(0)
            queries(0)
            norms(0, 1)
            recips(0, 0)
            recips(0, 1)
            attended(0, nxt=1)
            keys(1, 0)
            queries(1, routed=0)
            with act.Fori(1, B - 1) as b:
                experts(b - 1, during=b)
                attended(b, b - 1, b - 1, b + 1)
                keys(b + 1, b, b - 1)
                queries(b + 1, b - 1, b)
            norms(B - 1, 1)
            recips(B - 1, 0)
            recips(B - 1, 1)
            attended(B - 1, scattered=B - 2)
            experts(B - 2, routed=B - 1)
            experts(B - 1, combined=B - 2)
            act.wait_ge(sm["res_ready"], B - 1)
            for g in range(G):
                weigh(B - 1, g, 1)

        @block.vector
        def _(dve):
            n = [0]

            def link(ins):
                n[0] += 1
                ins.then_inc(dve_chain, 1)
                dve.wait_ge(dve_chain, n[0])

            def rows(ap2d, k=T):
                return ap2d.unsqueeze(1).to_broadcast([P, k, P])

            def modrow(b, k):
                return rows(mod[:, bass.ds(b * (6 * P) + k * P, P)])

            def statistics(k, src, first_tile=0):
                stats, mv, var_e, _, _ = norm_of[k]
                for t in range(first_tile, T):
                    ins = dve.bn_stats(stats[:, t, :], src[:, t, :])
                link(ins)
                for t in range(T):
                    ins = dve.bn_aggr(mv[:, t, :], stats[:, t, :])
                link(ins)
                dve.tensor_scalar(var_e[:, :], mv[:, :, 1], EPS, None, ALU.add).then_inc(sm[f"var{k}"], 1)

            def normalise(k, b, dst, src):
                _, mv, _, rstd, _ = norm_of[k]
                dve.wait_ge(sm[f"rstd{k}"], b + 1)
                for t in range(T):
                    ins = dve.tensor_scalar(dst[:, t, :], src[:, t, :], mv[:, t, 0:1], rstd[:, t:t + 1],
                                            ALU.subtract, ALU.mult)
                return ins

            dve.memset(wo_bd[:, :, :], 0.0).then_inc(wo_zeroed, 1)
            dve.memset(hs[:, :, :], 0.0).then_inc(hs_zeroed, 1)
            dve.wait_ge(const_ready, 1)
            dve.tensor_copy(sel[:, :, :], sel_f[:, :, :]).then_inc(sel_ready, 1)
            dve.wait_ge(sm["x_in"], 16)
            statistics(1, x_first)
            normalise(1, 0, x_first, x_first).then_inc(sm["x_used"], 1)
            dve.memset(picks_bf[:, :, :], 0.0)
            dve.memset(ks_parts[:, :, :].bitcast(F32), 0.0)
            link(dve.tensor_tensor(fold[:, :], ident[0:2 * H, 0:H], ident[0:2 * H, H:2 * H], ALU.add))
            dve.memset(owner[:, S:], 0.0)
            for k in range(8):
                dve.memset(octal[:, :, k:k + 1], float(E ** k))
            link(dve.memset(recip[:, :, :], 0.0))
            dve.wait_ge(in_rows, 16 * 6)
            dve.wait_ge(su_act, 2 + 6 + 2 * B)
            mod_v = mod[:, :].rearrange("p (b k c) -> p b k c", b=B, k=6)

            def gate_of(v, sign):
                link(dve.tensor_scalar(sign, v, 0.0, 2.0, ALU.is_ge, ALU.mult))
                link(dve.tensor_scalar(sign, sign, -1.0, None, ALU.add))
                link(dve.tensor_tensor(v, v, sign, ALU.mult))
                link(dve.scalar_tensor_tensor(v, v, 0.25, sign, ALU.max, ALU.mult))

            for k in (1, 4):
                ins = dve.tensor_scalar(mod_v[:, :, k, :], mod_v[:, :, k, :], 1.0, None, ALU.add)
            link(ins)

            def rest(j, dst, hi):
                dve.wait_ge(su_act, j + 1)
                dve.tensor_tensor(dst, bank[j % 8][:, :], hi.bitcast(F32), ALU.subtract).then_inc(su_dve, 1)

            j0 = 2 + 6 + 2 * B
            for k in range(4):
                o = (k % 2) * 512
                rest(j0 + k, wqk_lo[:, k // 2, o:o + 512], wqk_hi[:, k // 2, o:o + 512])
            dve.wait_ge(su_act, j0 + 8)
            dve.wait_ge(sm["x_used"], 1)
            link(dve.tensor_tensor(x_first[:, :, :], x_first[:, :, :], modrow(0, 1), ALU.mult))
            dve.tensor_tensor(h_sb[:, :, :], x_first[:, :, :], modrow(0, 0), ALU.add).then_inc(sm["h_ready"], 1)
            for e in range(E):
                if e == E // 2:
                    for g in range(G):
                        rest(j0 + 8 + e + g, ht_lo[:, g * 512:g * 512 + 512], ht_hi[:, g * 512:g * 512 + 512])
                j = j0 + 8 + e + (G if e >= E // 2 else 0)
                rest(j, wgu_lo[:, e * 512:e * 512 + 512], wgu_hi[:, e * 512:e * 512 + 512])

            def norm1(b, part):
                stats, mv, var_e, rstd, _ = norm_of[1]
                if part == 0:
                    dve.wait_ge(sm["x_in"], b * 32)
                if part < 2:
                    for t in range(4 * part, 4 * part + 4):
                        ins = dve.bn_stats(stats[:, t, :], x_sb[:, t, :])
                    if part == 1:
                        link(ins)
                elif part == 2:
                    for t in range(T):
                        ins = dve.bn_aggr(mv[:, t, :], stats[:, t, :])
                    link(ins)
                    dve.tensor_scalar(var_e[:, :], mv[:, :, 1], EPS, None, ALU.add).then_inc(sm["var1"], 1)
                elif part < 7:
                    if part == 3:
                        dve.wait_ge(sm["rstd1"], b + 1)
                    for t in range(2 * (part - 3), 2 * (part - 3) + 2):
                        ins = dve.tensor_scalar(h_sb[:, t, :], x_sb[:, t, :], mv[:, t, 0:1], rstd[:, t:t + 1],
                                                ALU.subtract, ALU.mult)
                    if part == 6:
                        ins.then_inc(sm["x_used"], 1)
                elif part == 7:
                    dve.wait_ge(sm["x_used"], b + 1)
                    dve.tensor_tensor(h_sb[:, :, :], h_sb[:, :, :], modrow(b, 1), ALU.mult).then_inc(sm["h_scaled"], 1)
                else:
                    dve.wait_ge(sm["h_scaled"], b)
                    dve.tensor_tensor(h_sb[:, :, :], h_sb[:, :, :], modrow(b, 0), ALU.add).then_inc(sm["h_ready"], 1)

            def h_rest(b, *groups):
                for g in groups:
                    dve.wait_ge(sm["ht_act"], b * G - G + g + 1)
                    o = g * 512
                    dve.tensor_tensor(ht_lo[:, o:o + 512], bank[HB[g]][:, :], ht_hi[:, o:o + 512].bitcast(F32),
                                      ALU.subtract).then_inc(sm["ht_dve"], 1)

            def wide(ap, k=E):
                return ap.unsqueeze(2).to_broadcast([P, ap.shape[1], k])

            def picks(b):
                dve.wait_ge(sm["logit_full"], b + 1)
                link(dve.tensor_copy(logit[:, :, :], bank[7][:, 0:T * E].rearrange("p (t e) -> p t e", e=E)))
                for top, pick in ((top1, pick1), (top2, pick2)):
                    link(dve.tensor_reduce(top[:, :], logit[:, :, :], AX_X, ALU.max))
                    link(dve.tensor_tensor(eq[:, :, :], logit[:, :, :], wide(top[:, :]), ALU.is_equal))
                    link(dve.scalar_tensor_tensor(code[:, :, :], eq[:, :, :], -float(E), iota_e[:, :, :],
                                                  ALU.mult, ALU.add))
                    link(dve.tensor_reduce(first[:, :], code[:, :, :], AX_X, ALU.min))
                    link(dve.tensor_tensor(pick[:, :, :], code[:, :, :], wide(first[:, :]), ALU.is_equal))
                    if top is top1:
                        link(dve.scalar_tensor_tensor(logit[:, :, :], pick[:, :, :], -BIG, logit[:, :, :],
                                                      ALU.mult, ALU.add))
                dve.tensor_tensor(picks_bf[:, T - 1:, :], pick1[:, :, :], pick2[:, :, :], ALU.add
                                  ).then_inc(sm["picks_ready"], 1)
                dve.tensor_tensor(gap[:, :], top2[:, :], top1[:, :], ALU.subtract).then_inc(sm["gap_ready"], 1)

            def route(b, end=0):
                dve.wait_ge(sm["rank_full"], b + 1)
                count = bank[6][:, 0:E].unsqueeze(2).to_broadcast([P, E, T])
                link(dve.tensor_tensor(over[:, :, :], count, step128[:, :, :], ALU.is_gt))
                link(dve.tensor_reduce(n_tiles[:, :], over[:, :, :], AX_X, ALU.add))
                link(dve.tensor_tensor(prior[:, :, :], before[:, :, :],
                                       n_tiles[:, :].unsqueeze(1).to_broadcast([P, E, E]), ALU.mult))
                link(dve.tensor_reduce(tile0[:, :], prior[:, :, :], AX_X, ALU.add))
                link(dve.scalar_tensor_tensor(slot[:, :, :], tile0[:, :].unsqueeze(1).to_broadcast([P, T, E]),
                                              float(P), bank[7][:, 64:128].rearrange("p (t e) -> p t e", e=E),
                                              ALU.mult, ALU.add))
                for k, pick in enumerate((pick1, pick2)):
                    link(dve.tensor_tensor(slot_p[:, :, :], slot[:, :, :], pick[:, :, :], ALU.mult))
                    link(dve.tensor_reduce(slots[:, k * T:(k + 1) * T], slot_p[:, :, :], AX_X, ALU.add))
                dve.tensor_copy(slots_i[:, end, :], slots[:, :]).then_inc(sm["route_ready"], 1)
                link(dve.tensor_tensor(tile1[:, :], tile0[:, :], n_tiles[:, :], ALU.add))
                link(dve.tensor_tensor(passed[:, :, :], tile1[:, :].unsqueeze(1).to_broadcast([P, S, E]),
                                       iota_s[:, :, :], ALU.is_le))
                link(dve.tensor_reduce(owner[:, 0:S], passed[:, :, :], AX_X, ALU.add))
                link(dve.scalar_tensor_tensor(coded[:, :, :], owner[:, :].rearrange("p (w k) -> p w k", k=8),
                                              float(E - 1), octal[:, :, :], ALU.min, ALU.mult))
                link(dve.tensor_reduce(owners[:, :], coded[:, :, :], AX_X, ALU.add))
                dve.tensor_copy(owners_i[:, end, :], owners[:, :]).then_inc(sm["owner_ready"], 1)
                dve.wait_ge(sm["tanh_done"], b + 1)
                dve.tensor_scalar(w2[:, end, :], th[:, :], 0.5, 0.5, ALU.mult, ALU.add)
                dve.tensor_scalar(w1[:, end, :], th[:, :], -0.5, 0.5, ALU.mult, ALU.add).then_inc(sm["w_ready"], 1)

            def shift(k, b):
                _, mv, _, rstd, shift_k = norm_of[k]
                dve.wait_ge(sm[f"rstd{k}"], b + 1)
                dve.scalar_tensor_tensor(shift_k[:, :], mv[:, :, 0], -1.0, rstd[:, :], ALU.mult, ALU.mult
                                         ).then_inc(sm[f"shift{k}"], 1)

            def norm2(b, part, src=x2):
                if part == 0:
                    dve.wait_ge(sm["x2_ready"], b * G + G)
                    statistics(2, src)
                else:
                    if part == 1:
                        link(normalise(2, b, h2, src))
                    else:
                        dve.wait_ge(sm["normed2"], b + 1)
                    link(dve.tensor_tensor(h2[:, :, :], h2[:, :, :], modrow(b, 4), ALU.mult))
                    dve.tensor_tensor(h2[:, :, :], h2[:, :, :], modrow(b, 3), ALU.add).then_inc(sm["h2_ready"], 1)

            def keys(b, routed=None, combined=None, normed=None):
                bias = bf_row[:, :].unsqueeze(1).to_broadcast([P, 512 // D, D])
                for i in range(2 * T):
                    t = i // 2
                    if combined is not None and i == 1:
                        weigh(combined, halves=(1,))
                    dve.wait_ge(sm["k_full"], b * 2 * T + i + 1)
                    if i % 2 == 0 and t >= 2:
                        dve.wait_ge(sm["g_done"], b * T + t - 1)
                        dve.wait_ge(sm["k_added"], b * (T - 1) + max(1, t - 2))
                    dst = kf[:, t % 2, (i % 2) * 512:(i % 2) * 512 + 512]
                    dve.tensor_tensor(dst.rearrange("p (h d) -> p h d", d=D),
                                      bank[Z[i % 3]][:, :].rearrange("p (h d) -> p h d", d=D), bias, ALU.add
                                      ).then_inc(sm["k_biased"], 1)
                    if i % 2 and routed is not None:
                        if t == 0:
                            norm2(routed, 0)
                        elif t == 1:
                            shift(2, routed)
                        elif t == 2:
                            norm2(routed, 2)
                        elif t == 5:
                            picks(routed)
                        elif t == T - 1:
                            route(routed)
                    if i % 2 and normed is not None and 2 <= t < 5:
                        norm1(normed, t - 2)
                    if normed is not None and i == 11:
                        gate_of(mod_v[:, :, 5, :], sign_b)
                    elif normed is not None and i == 12:
                        link(dve.tensor_tensor(mod_v[:, :, 2, :], mod_v[:, :, 5, :], rows(gamma_row[:, :], B),
                                               ALU.mult))
                        dve.tensor_tensor(mod_v[:, :, 5, :], mod_v[:, :, 5, :], rows(beta_row[:, :], B), ALU.mult)
                    elif normed is not None and i == 13:
                        gate_of(ga_col[:, :, 0], th[:, 0:B])
                        link(dve.tensor_scalar(ga_col[:, :, 1], ga_col[:, :, 0], bout_col[:, 0:1], None, ALU.mult))
                    if i % 2 and combined is not None:
                        if t == 1:
                            statistics(3, y)
                        elif t == 3:
                            shift(3, combined)
                        elif t == 6:
                            dve.wait_ge(sm["normed3"], combined + 1)
                            dve.tensor_tensor(y[:, :, :], y[:, :, :], modrow(combined, 2), ALU.mult
                                              ).then_inc(sm["y_modulated"], 1)

            def keys_by_head(b):
                dve.wait_ge(sm["ksum_full"], b + 1)
                link(dve.tensor_tensor(ks_bd[:, :, :], head_mask[:, :, :],
                                       bank[5][:, 0:NJ].unsqueeze(2).to_broadcast([P, NJ, H]), ALU.mult))
                link(dve.tensor_copy(ks_parts[:, :, H:2 * H], ks_bd[:, :, :]))
                dve.tensor_tensor(ks_parts[:, :, 0:H], ks_bd[:, :, :], ks_parts[:, :, H:2 * H].bitcast(F32),
                                  ALU.subtract).then_inc(sm["ks_ready"], 1)

            def rows_rest(b, q):
                w = len(quad(q)) * P
                dve.wait_ge(sm["ft_hi"], b * NQ + q + 1)
                dve.tensor_tensor(hst_lo[:, q % 2, 0:w], bank[FT][:, 0:w], hst_hi[:, q % 2, 0:w].bitcast(F32),
                                  ALU.subtract).then_inc(sm["ft_lo"], 1)

            def queries(b, normed=None, routed=None):
                link(dve.tensor_copy(ga_now[:, :], ga_col[:, :, :].rearrange("p b k -> p (b k)")[:, bass.ds(b * 2, 2)]))
                for i in range(G * NJ):
                    if i == 3:
                        for k in range(4):
                            if k == 2:
                                keys_by_head(b)
                            dve.wait_ge(sm["m_full"], b * 4 + k + 1)
                            mb = bank[MB[k]][:, :].rearrange("p (a s d) -> p a s d", a=2, s=2)
                            dve.tensor_copy(m_sb[0:D, 2 * k:2 * k + 2, :], mb[0:D, :, 0, :])
                            dve.tensor_copy(m_sb[D:P, 2 * k:2 * k + 2, :], mb[D:P, :, 1, :]).then_inc(sm["m_copied"], 1)
                    dve.wait_ge(sm["q_ready"], b * G * NJ + i + 1)
                    dve.tensor_tensor(q_part(i, 1), q_act[:, i // NJ, i % NJ, :], q_part(i, 0).bitcast(F32),
                                      ALU.subtract).then_inc(sm["q_lo"], 1)
                    if normed is not None and i % 2 and 3 <= i < 15:
                        norm1(normed, 3 + i // 2 - 1)
                if routed is not None:
                    rows_rest(routed, 0)

            def recips(b, g):
                dve.wait_ge(sm["normt_full"], b * G + g + 1)
                link(dve.tensor_scalar(recip_in[:, :, :],
                                       bank[6 + g][:, 0:4 * H].rearrange("p (t h) -> p t h", h=H),
                                       1e-6, None, ALU.add))
                link(dve.reciprocal(recip[:, :, 0:H], recip_in[:, :, :]))
                dve.tensor_copy(recip[:, :, 32:32 + H], recip[:, :, 0:H]).then_inc(sm["r_ready"], 1)

            def recips_rest(b, g):
                dve.wait_ge(sm["r_hi"], b * G + g + 1)
                dve.tensor_tensor(r_parts[32:64, g, :], bank[6 + g][32:64, :], r_parts[32:64, g, :].bitcast(F32),
                                  ALU.subtract).then_inc(sm["r_lo"], 1)

            def experts(b, src=x2, end=0, during=None, routed=None, combined=None):
                if end:
                    rows_rest(b, 0)
                for i in range(S + 2):
                    if i < S:
                        if i % 4 == 0 and i // 4 + 1 < NQ:
                            rows_rest(b, i // 4 + 1)
                        dve.wait_ge(sm["silu_done"], b * S + i + 1)
                        if i >= 2:
                            dve.wait_ge(sm["hidt_full"], b * S + i - 1)
                        dve.tensor_tensor(hid[:, i % 2, :], bank[i % 2][:, F:2 * F], gate[:, i % 2, :], ALU.mult
                                          ).then_inc(sm["hid_ready"], 1)
                    if i >= 2:
                        dve.wait_ge(sm["y_full"], b * S + i - 1)
                        if end and i == 2:
                            dve.wait_ge(sm["y_stored"], b * (16 * NQ))
                        dve.tensor_copy(y_sb[:, i - 2, :], bank[YB[i % 2]][:, 0:P]).then_inc(sm["y_copied"], 1)
                    if during is not None:
                        if i == 0:
                            recips(during, 0)
                        elif i == 2:
                            recips_rest(during, 0)
                        elif i == 3:
                            recips(during, 1)
                        elif i == 5:
                            recips_rest(during, 1)
                        if 6 <= i < 15:
                            norm1(during + 1, i - 6)
                    if i == (20 if end else 17):
                        onto_x2(b, src)
                    if routed is not None:
                        if i == 0:
                            norm2(routed, 0, x2_end)
                        elif i == 1:
                            norm2(routed, 1, x2_end)
                        elif i == 7:
                            picks(routed)
                        elif i == 10:
                            route(routed, 1)
                    if combined is not None:
                        if i in (10, 11):
                            weigh(combined, halves=(i - 10,))
                        elif i == 12:
                            statistics(3, y)
                        elif i == 14:
                            normalise_y(combined)
                        elif i == 16:
                            finish(combined)

            def onto_x2(b, src):
                dve.wait_ge(sm["stored"], b * 16 + 16)
                dve.tensor_tensor(res[:, :, :], src[:, :, :], modrow(b, 5), ALU.add)

            def weigh(b, end=0, halves=range(G)):
                dve.wait_ge(sm["w_ready"], b + 1)
                for g in halves:
                    dve.wait_ge(sm["y1_weighed"], b * G + g + 1)
                    dve.wait_ge(gathered[g], b * (16 * T) + 16 * T)
                    for t in range(4 * g, 4 * g + 4):
                        ins = dve.scalar_tensor_tensor(y[:, t, :], y2[:, t, :], w2[:, end, t:t + 1], y[:, t, :],
                                                       ALU.mult, ALU.add)
                    ins.then_inc(sm["y_taken"], 1)
                    dve.wait_ge(sm["y_taken"], b * G + g + 1)

            def normalise_y(b):
                link(normalise(3, b, y, y))
                link(dve.tensor_tensor(y[:, :, :], y[:, :, :], modrow(b, 2), ALU.mult))

            def finish(b):
                dve.tensor_tensor(res[:, :, :], y[:, :, :], res[:, :, :], ALU.add).then_inc(sm["res_ready"], 1)

            def residual(b, g, dst, end):
                if g == 0:
                    dve.wait_ge(sm["x_in"], 32 * B if end else b * 32 + 48)
                dve.wait_ge(sm["att_full"], b * G + g + 1)
                dve.tensor_tensor(dst[:, 4 * g:4 * g + 4, :], bank[6 + g][:, :].rearrange("p (t c) -> p t c", c=P),
                                  x_sb[:, 4 * g:4 * g + 4, :], ALU.add).then_inc(sm["x2_ready"], 1)

            def attended(b, dst=x2, combined=None, nxt=None, end=False):
                for g in range(G):
                    for j in range(NJ):
                        i = NJ * g + j
                        if nxt is not None and i in (3, 5):
                            h_rest(nxt, i // 5)
                        if i == 14:
                            residual(b, 0, dst, end)
                        dve.wait_ge(sm["rb_full"], b * G * NJ + i + 1)
                        if i >= 2:
                            dve.wait_ge(sm["out_done"], b * G * NJ + i - 1)
                        dve.tensor_tensor(qn[:, i % 2, :], bank[2 + i % 2][:, :], q_act[:, g, j, :], ALU.mult
                                          ).then_inc(sm["qn_ready"], 1)
                if combined is not None:
                    weigh(combined, halves=(0,))
                residual(b, 1, dst, end)

            keys(0, normed=1)
            queries(0, normed=1)
            for g in range(G):
                recips(0, g)
                recips_rest(0, g)
            attended(0, nxt=1)
            keys(1, routed=0)
            queries(1, routed=0)
            with dve.Fori(1, B - 1) as b:
                dve.sem_clear(dve_chain)
                n[0] = 0
                experts(b - 1, during=b)
                attended(b, combined=b - 1, nxt=b + 1)
                keys(b + 1, routed=b, combined=b - 1)
                queries(b + 1, routed=b)
            dve.sem_clear(dve_chain)
            n[0] = 0
            for g in range(G):
                recips(B - 1, g)
                recips_rest(B - 1, g)
            attended(B - 1, dst=x2_end, end=True)
            experts(B - 2, routed=B - 1)
            experts(B - 1, src=x2_end, end=1, combined=B - 2)
            weigh(B - 1, 1, (0,))
            for t in range(T // 2):
                dve.bn_stats(norm_of[3][0][:, t, :], y[:, t, :])
            weigh(B - 1, 1, (1,))
            statistics(3, y, first_tile=T // 2)
            normalise_y(B - 1)
            finish(B - 1)

        @block.tensor
        def _(pe):
            job = [0]
            splits = []

            def take():
                k = job[0] - 8
                if k >= 0:
                    pe.wait_ge(su_act, k + 1)
                    if k in splits:
                        pe.wait_ge(su_dve, splits.index(k) + 1)
                job[0] += 1
                return bank[(job[0] - 1) % 8]

            pe.wait_ge(ident_ready, 1)
            pe.wait_ge(in_cond, 48)
            bk = take()
            pe.transpose(bk[:, 0:E], wr_nat[:, :], ident[0:E, 0:E])
            pe.transpose(bk[:, 16:16 + B], c_nat[:, :], ident[0:B, 0:B]).then_inc(su_full, 1)
            pe.wait_ge(su_act, 1)
            bk = take()
            pe.matmul(bk[:, 0:B], wmod_sb[:, 2 * P:3 * P], c_t[:, :], start=True, stop=True).then_inc(su_full, 1)
            pe.wait_ge(in_qkv, 16)
            for k in range(6):
                bk = take()
                for i in range(4):
                    o = (4 * k + i) * P
                    ins = pe.transpose(bk[:, i * P:(i + 1) * P], wqkv_nat[:, o:o + P], ident[:, :])
                ins.then_inc(su_full, 1)
            pe.wait_ge(c_wide, B)
            for k in range(2 * B):
                bk = take()
                o = (k % 2) * 384
                pe.matmul(bk[:, 0:384], c_b[:, k // 2, :], wmod_sb[:, o:o + 384], start=True, stop=True
                          ).then_inc(su_full, 1)
            pe.wait_ge(su_act, 8)
            pe.wait_ge(in_heads, 64)
            for k in range(4):
                splits.append(job[0])
                bk = take()
                for i in range(4):
                    ins = pe.matmul(bk[:, i * P:(i + 1) * P], wt[:, 4 * k + i, :], wf_bd[:, :], start=True, stop=True)
                ins.then_inc(su_full, 1)
            for k in range(4):
                bk = take()
                for i in range(2):
                    j = 2 * k + i
                    ins = pe.matmul(bk[:, i * 256:(i + 1) * 256], wt[:, 16 + j, :], wo_bd[:, j, :],
                                    start=True, stop=True)
                ins.then_inc(su_full, 1)
            pe.wait_ge(in_gu, 32)
            for e in range(E):
                if e == E // 2:
                    pe.wait_ge(sm["h_ready"], 1)
                    for g in range(G):
                        splits.append(job[0])
                        bk = take()
                        for i in range(4):
                            ins = pe.transpose(bk[:, i * P:(i + 1) * P], h_sb[:, 4 * g + i, :], ident[:, :])
                        ins.then_inc(su_full, 1)
                splits.append(job[0])
                bk = take()
                for i in range(4):
                    src = (wg_nat, wu_nat)[i // 2][:, 2 * e + i % 2, :]
                    ins = pe.transpose(bk[:, i * P:(i + 1) * P], src, ident[:, :])
                ins.then_inc(su_full, 1)
            pe.wait_ge(in_down, 16)
            for k in range(4):
                bk = take()
                for i in range(4):
                    e, f = 2 * k + i // 2, i % 2
                    ins = pe.transpose(bk[:, i * P:(i + 1) * P], wd_nat[:, e, f * P:(f + 1) * P], ident[:, :])
                ins.then_inc(su_full, 1)
            pe.wait_ge(su_act, job[0])
            pe.wait_ge(su_dve, 4 + E + G)
            pe.wait_ge(const_ready, 1)
            pe.wait_ge(sel_ready, 1)

            def product(dst, hi, lo, rhs_hi, rhs_lo):
                pe.matmul(dst, hi, rhs_hi, start=True, stop=False)
                pe.matmul(dst, hi, rhs_lo, start=False, stop=False)
                return pe.matmul(dst, lo, rhs_hi, start=False, stop=True)

            def transposes(b, ready, src, full, banks):
                pe.wait_ge(sm[ready], b + 1)
                for g in range(G):
                    for i in range(4):
                        ins = pe.transpose(bank[banks[g]][:, i * P:(i + 1) * P], src[:, 4 * g + i, :], ident[:, :])
                    ins.then_inc(sm[full], 1)

            def key_features(b, i):
                if i >= 3:
                    pe.wait_ge(sm["k_biased"], b * 2 * T + i - 2)
                tok, o = slice(i // 2 * P, (i // 2 + 1) * P), slice(i % 2 * 512, i % 2 * 512 + 512)
                product(bank[Z[i % 3]][:, :], ht_hi[:, tok], ht_lo[:, tok], wqk_hi[:, 1, o], wqk_lo[:, 1, o]
                        ).then_inc(sm["k_full"], 1)

            def keys(b, routed=None, begun=True):
                for t in range(T + 1):
                    if t < T:
                        for i in (2 * t, 2 * t + 1):
                            if i or not begun:
                                key_features(b, i)
                    if routed is not None and t == 4:
                        transposes(routed, "h2_ready", h2, "h2t_full", (6, 7))
                    if routed is not None and t == 5:
                        logits(routed)
                    if routed is not None and t == 7:
                        ranks(routed)
                    if t >= 1:
                        pe.wait_ge(sm["k_relu"], b * 2 * T + 2 * t)
                        for k in range(2):
                            ins = pe.matmul(bank[2 + k][:, :], h_sb[:, t - 1, :],
                                            kf[:, (t - 1) % 2, k * 512:k * 512 + 512], start=t == 1, stop=t == T)
                        ins.then_inc(sm["g_done"], 1)

            def logits(b):
                pe.wait_ge(sm["h2t_copied"], b * G + G)
                for t in range(T):
                    ins = pe.matmul(bank[7][:, t * E:(t + 1) * E], h2t[:, t * P:(t + 1) * P], wr_t[:, :],
                                    start=True, stop=True)
                ins.then_inc(sm["logit_full"], 1)

            def ranks(b):
                pe.wait_ge(sm["picks_ready"], b + 1)
                rank = bank[7][:, 64:128]
                pe.matmul(rank, lower_bf[:, :], picks_bf[:, T - 1:, :], start=True, stop=False)
                for back in range(1, T):
                    pe.matmul(rank, ones_bf[:, :], picks_bf[:, T - 1 - back:2 * T - 1 - back, :], start=False,
                              stop=back == T - 1)
                for t in range(T):
                    ins = pe.matmul(bank[6][:, 0:E], ones_bf[:, :], picks_bf[:, T - 1 + t, :], start=t == 0,
                                    stop=t == T - 1)
                ins.then_inc(sm["rank_full"], 1)

            def q_features(b, i):
                if i >= 3:
                    pe.wait_ge(sm["q_ready"], b * G * NJ + i - 2)
                g, j = divmod(i, NJ)
                f, tok = slice(j * P, (j + 1) * P), slice(g * 512, g * 512 + 512)
                product(bank[Z[i % 3]][:, :], wqk_hi[:, 0, f], wqk_lo[:, 0, f], ht_hi[:, tok], ht_lo[:, tok]
                        ).then_inc(sm["q_full"], 1)

            def normaliser(b, i):
                g, j = divmod(i, NJ)
                dst = bank[NB[g]][0:2 * H, :]
                pe.wait_ge(sm["q_lo"], b * G * NJ + i + 1)
                pe.matmul(dst, ks_parts[:, j, 0:2 * H], q_part(i, 0), start=j == 0, stop=False)
                pe.matmul(dst, ks_parts[:, j, H:3 * H], q_part(i, 1), start=False, stop=j == NJ - 1
                          ).then_inc(sm["q_normed"], 1)

            def norms_t(b, g):
                pe.wait_ge(sm["norm_copied"], b * G + g + 1)
                for i in range(4):
                    ins = pe.matmul(bank[6 + g][:, H * i:H * i + H], norm_sb[:, i * P:(i + 1) * P], fold[:, :],
                                    start=True, stop=True)
                ins.then_inc(sm["normt_full"], 1)

            def recips_t(b, g):
                pe.wait_ge(sm["r_ready"], b * G + g + 1)
                pe.transpose(bank[6 + g][0:32, 0:P], recip[:, 0, 0:32], ident[:, :])
                for i in range(4):
                    ins = pe.transpose(bank[6 + g][0:64, i * P:(i + 1) * P], recip[:, i, :], ident[:, :])
                ins.then_inc(sm["rt_full"], 1)

            def rows_t(b, q, src=hs):
                pe.wait_ge(hs_in[q], b * 16 + 16)
                if q >= 1:
                    pe.wait_ge(sm["ft_lo"], b * NQ + q)
                for i, s in enumerate(quad(q)):
                    ins = pe.transpose(bank[FT][:, i * P:(i + 1) * P], src[:, s, :], ident[:, :])
                ins.then_inc(sm["ft_full"], 1)

            def keys_summed(b):
                pe.wait_ge(sm["k_added"], b * (T - 1) + T - 1)
                for j in range(NJ):
                    ins = pe.matmul(bank[5][:, j:j + 1], k_sum[:, j * P:(j + 1) * P], ones_col[:, :],
                                    start=True, stop=True)
                ins.then_inc(sm["ksum_full"], 1)

            def queries(b, routed=None):
                for i in range(3):
                    q_features(b, i)
                pe.wait_ge(sm["gt_copied"], b * 2 + 2)
                for k in range(4):
                    if k == 2:
                        keys_summed(b)
                    if k == 0 and routed is not None:
                        pe.wait_ge(sm["route_ready"], routed + 1)
                    for i in range(2):
                        j = 2 * k + i
                        ins = pe.matmul(bank[MB[k]][:, i * 256:(i + 1) * 256], gt_sb[:, j * P:(j + 1) * P],
                                        vo[:, 2 * j:2 * j + 2, :], start=True, stop=True)
                    ins.then_inc(sm["m_full"], 1)
                for i in range(3, G * NJ + 3):
                    if i < G * NJ:
                        q_features(b, i)
                    if i == 3:
                        pe.wait_ge(sm["ks_ready"], b + 1)
                    if i == 11:
                        pe.wait_ge(sm["m_copied"], b * 4 + 4)
                    if i == G * NJ + 1 and routed is not None:
                        pe.wait_ge(sm["owner_ready"], routed + 1)
                        rows_t(routed, 0)
                    normaliser(b, i - 3)
                    if i == 12:
                        norms_t(b, 0)

            def next_tokens(b):
                pe.wait_ge(sm["r_lo"], b * G)
                transposes(b, "h_ready", h_sb, "ht_full", HB)

            def attention_t(b, g):
                pe.wait_ge(sm["at_copied"], b * G + g + 1)
                for i in range(4):
                    ins = pe.transpose(bank[6 + g][:, i * P:(i + 1) * P], at_sb[:, g, i * P:(i + 1) * P], ident[:, :])
                ins.then_inc(sm["att_full"], 1)

            def attend(b, nxt=None):
                for i in range(G * NJ + 1):
                    if i < G * NJ:
                        if i % NJ == 0:
                            pe.wait_ge(sm["r_lo"], b * G + i // NJ + 1)
                        if i >= 2:
                            pe.wait_ge(sm["qn_ready"], b * G * NJ + i - 1)
                        pe.matmul(bank[2 + i % 2][:, :], sel[0:64, i % NJ, :], r_parts[0:64, i // NJ, :], start=True,
                                  stop=True).then_inc(sm["rb_full"], 1)
                    if i == 12 and nxt is not None:
                        pe.wait_ge(sm["ht_dve"], nxt * G)
                    if i == 1 and nxt is not None:
                        next_tokens(nxt)
                    if i >= 1:
                        g, j = divmod(i - 1, NJ)
                        pe.wait_ge(sm["qn_ready"], b * G * NJ + i)
                        pe.matmul(bank[4 + g][:, :], m_sb[:, j, :], qn[:, (i - 1) % 2, :], start=j == 0,
                                  stop=j == NJ - 1).then_inc(sm["out_done"], 1)
                    if i == 12:
                        attention_t(b, 0)
                if nxt is not None:
                    key_features(nxt, 0)
                attention_t(b, 1)

            def experts(b, src=hs, end=0, during=None, routed=None):
                def experts_of(w):
                    return pe.value_load(owners_i[0:1, end, w:w + 1], min_val=0, max_val=E ** 8 - 1)

                if end:
                    pe.wait_ge(sm["owner_ready"], b + 1)
                    rows_t(b, 0, src)
                word = experts_of(0)
                expert = {}
                for i in range(S + 2):
                    if i < S:
                        if i % 4 == 0 and i // 4 + 1 < NQ:
                            pe.wait_ge(sm["ft_lo"], b * NQ + i // 4 + 1)
                            rows_t(b, i // 4 + 1, src)
                        pe.wait_ge(sm["ft_lo"], b * NQ + i // 4 + 1)
                        if i >= 2:
                            pe.wait_ge(sm["hid_ready"], b * S + i - 1)
                        tok = slice((i % 4) * P, (i % 4 + 1) * P)
                        expert[i] = ((word >> (3 * (i % 8))) if i % 8 else word) & (E - 1)
                        cols = bass.ds(expert[i] * (2 * F), 2 * F)
                        product(bank[i % 2][:, :], hst_hi[:, (i // 4) % 2, tok], hst_lo[:, (i // 4) % 2, tok],
                                wgu_hi[:, cols], wgu_lo[:, cols]).then_inc(sm["gu_full"], 1)
                        if i % 8 == 7:
                            word = experts_of(i // 8 + 1)
                    if 1 <= i <= S:
                        k = i - 1
                        pe.wait_ge(sm["hid_ready"], b * S + k + 1)
                        if k >= 1:
                            pe.wait_ge(sm["hidt_copied"], b * S + k)
                        for f in range(2):
                            ins = pe.transpose(bank[HT][:, f * P:(f + 1) * P],
                                               hid[:, k % 2, f * P:(f + 1) * P], ident[:, :])
                        ins.then_inc(sm["hidt_full"], 1)
                    if i >= 2:
                        k = i - 2
                        pe.wait_ge(sm["hidt_copied"], b * S + k + 1)
                        if k >= 2:
                            pe.wait_ge(sm["y_copied"], b * S + k - 1)
                        for f in range(2):
                            ins = pe.matmul(bank[YB[k % 2]][:, 0:P], hid_t[:, k % 2, f * P:(f + 1) * P],
                                            wd[:, bass.ds(expert[k] * (2 * P) + f * P, P)], start=f == 0, stop=f == 1)
                        ins.then_inc(sm["y_full"], 1)
                    if during is not None:
                        if i == 1:
                            norms_t(during, 1)
                        elif i == 2:
                            recips_t(during, 0)
                        elif i == 4:
                            recips_t(during, 1)
                    if routed is not None:
                        if i == 4:
                            transposes(routed, "h2_ready", h2, "h2t_full", (6, 7))
                        elif i == 6:
                            logits(routed)
                        elif i == 9:
                            ranks(routed)
                pe.wait_ge(sm["y_copied"], b * S + S)

            def reciprocals(b):
                recips_t(b, 0)
                norms_t(b, 1)
                recips_t(b, 1)

            keys(0, begun=False)
            queries(0)
            reciprocals(0)
            attend(0, nxt=1)
            keys(1, 0)
            queries(1, 0)
            with pe.Fori(1, B - 1) as b:
                experts(b - 1, during=b)
                attend(b, nxt=b + 1)
                keys(b + 1, b)
                queries(b + 1, b)
            reciprocals(B - 1)
            attend(B - 1)
            experts(B - 2, routed=B - 1)
            experts(B - 1, src=hs_end, end=1)


_INS = ['L0_attn_x', 'L0_attn_W_qkv', 'L0_attn_W_f', 'L0_attn_b_f', 'L0_attn_W_out', 'L0_attn_b_out',
        'L0_ffn_w_router', 'L0_ffn_w_gate', 'L0_ffn_w_up', 'L0_ffn_w_down', 'L0_ffn_ln_gamma', 'L0_ffn_ln_beta',
        'L0_c', 'L0_wmod']


def kernel(**inputs):
    import numpy as np
    import concourse.bacc as bacc
    from concourse import mybir as mb
    from concourse.bass_utils import run_bass_kernel_spmd

    nc = bacc.Bacc("TRN2", target_bir_lowering=False, num_devices=1)
    arrays, args = {}, []
    for name in _INS:
        a = np.ascontiguousarray(inputs[name])
        arrays[f"in_{name}"] = a
        args.append(nc.dram_tensor(f"in_{name}", a.shape, mb.dt.from_np(a.dtype), kind="ExternalInput").ap())
    shape = inputs['L0_attn_x'].shape
    args.append(nc.dram_tensor("out_x", shape, mb.dt.float32, kind="ExternalOutput").ap())
    build_block(nc, *args)
    r = run_bass_kernel_spmd(nc, [arrays], core_ids=[0])
    return r.results[0]["out_x"]
```
